# Optimizing a Trainium2 kernel written in Bass

```python
import numpy as np
import jax
import jax.numpy as jnp

def _softmax(x, axis=-1):
    return jax.nn.softmax(x, axis=axis)

def _gelu(x):
    return jax.nn.gelu(x, approximate=True)

def _silu(x):
    return jax.nn.silu(x)

def _sigmoid(x):
    return jax.nn.sigmoid(x)

def _layernorm(x, axis=-1, eps=1e-05):
    m = jnp.mean(x, axis=axis, keepdims=True)
    v = jnp.var(x, axis=axis, keepdims=True)
    return (x - m) / jnp.sqrt(v + eps)

def _scatter_add(tgt, idx, src, axis=0):
    return tgt.at[idx].add(src)

def _segment_sum(src, seg, n):
    return jax.ops.segment_sum(src, seg, n)
kernel_name = 'mk_xattn_ffn_d1_seqx_r4_e16d03'

def setup_inputs(seed: int=0):
    np.random.seed(seed)
    _w = jnp.asarray

    def _rec_inputs():
        import jax
        import jax.numpy as jnp
        _rk = jax.random.key(seed)
        x = -7.109e-05 + 0.9999 * jax.random.normal(jax.random.fold_in(_rk, 1), (4, 512, 512), jnp.float32)
        _lenS = 512 - jax.random.randint(jax.random.fold_in(_rk, 7), (4,), 0, max(1, 512 // 4) + 1, jnp.int32)
        _lenS2 = 512 - jax.random.randint(jax.random.fold_in(_rk, 8), (4,), 0, max(1, 512 // 4) + 1, jnp.int32)
        _ctx_2048P = jax.random.normal(jax.random.fold_in(_rk, 11), (4, 16, 512), jnp.float32)
        _ctx_2048c = jax.random.dirichlet(jax.random.fold_in(_rk, 511), 0.3 * jnp.ones((16,), jnp.float32), (4, 512))
        _ctx_2048t = jnp.einsum('bsk,bkd->bsd', _ctx_2048c, _ctx_2048P)
        _ctx_2048t = _ctx_2048t * jax.lax.rsqrt(jnp.mean(jnp.square(_ctx_2048t)) + 1e-12) * 0.953939
        ctx_2048 = -3.05549e-07 + 0.0199987 * (_ctx_2048t + 0.3 * jax.random.normal(jax.random.fold_in(_rk, 611), (4, 512, 512), jnp.float32))
        return (x, ctx_2048)
    x, ctx_2048 = _rec_inputs()

    def _L0_xattn_setup():
        import jax, jax.numpy as jnp
        import numpy as np
        FP8_MAX = 448.0
        ACT_EPS = 0.0001
        W_EPS = 1e-06
        BLK = 128

        def quant_dequant_act_1x128(x):
            E, M, K = x.shape
            xb = x.reshape(E, M, K // BLK, BLK)
            amax = jnp.max(jnp.abs(xb), axis=-1, keepdims=True)
            safe = jnp.maximum(amax, ACT_EPS)
            q = (xb * (FP8_MAX / safe)).astype(jnp.float8_e4m3fn)
            return (q.astype(jnp.float32) * (safe / FP8_MAX)).reshape(E, M, K)

        def quant_dequant_weight_128x128(w):
            E, N, K = w.shape
            wb = w.reshape(E, N // BLK, BLK, K // BLK, BLK)
            amax = jnp.max(jnp.abs(wb), axis=(2, 4), keepdims=True)
            safe = jnp.maximum(amax, W_EPS)
            q = (wb * (FP8_MAX / safe)).astype(jnp.float8_e4m3fn)
            return (q.astype(jnp.float32) * (safe / FP8_MAX)).reshape(E, N, K)
        key = jax.random.key(seed)
        kx, kw = jax.random.split(key)
        E, M, K, N = (8, 1024, 512, 512)
        x = jax.random.normal(kx, (E, M, K), dtype=jnp.float32)
        weight = jax.random.normal(kw, (E, N, K), dtype=jnp.float32) * 0.02
        return {'x': x, 'weight': weight}
    _L0_xattn_all = _L0_xattn_setup()
    _L0_xattn_in = {k: v for k, v in _L0_xattn_all.items() if k in ()}
    del _L0_xattn_all

    def _L0_ffn_setup():
        import jax, jax.numpy as jnp
        import numpy as np
        H = 512
        I = 256
        K = 8
        E = 128
        TOPK = 4
        EPS = 1e-08
        key = jax.random.key(seed)
        ks = jax.random.split(key, 10)
        s = 0.02
        return {'x': jax.random.normal(ks[0], (4, 512, H), jnp.float32), 'w_router': jax.random.normal(ks[1], (H, E), jnp.float32) * s, 'w_gate': jax.random.normal(ks[2], (H, K * I), jnp.float32) * s, 'w_up': jax.random.normal(ks[3], (H, K * I), jnp.float32) * s, 'w_down': jax.random.normal(ks[4], (I, H), jnp.float32) * s, 'amplitudes': jax.random.normal(ks[5], (E, K, 2), jnp.float32) * 0.1, 'expert_scale': jnp.ones((E,), jnp.float32), 'shared_w_gate': jax.random.normal(ks[6], (H, 2 * I), jnp.float32) * s, 'shared_w_up': jax.random.normal(ks[7], (H, 2 * I), jnp.float32) * s, 'shared_w_down': jax.random.normal(ks[8], (2 * I, H), jnp.float32) * s}
    _L0_ffn_all = _L0_ffn_setup()
    _L0_ffn_in = {k: v for k, v in _L0_ffn_all.items() if k in ('w_router', 'w_gate', 'w_up', 'w_down', 'amplitudes', 'expert_scale', 'shared_w_gate', 'shared_w_up', 'shared_w_down')}
    del _L0_ffn_all
    return {'x': x, 'ctx_2048': ctx_2048, 'L0_ffn_w_router': _L0_ffn_in['w_router'], 'L0_ffn_w_gate': _L0_ffn_in['w_gate'], 'L0_ffn_w_up': _L0_ffn_in['w_up'], 'L0_ffn_w_down': _L0_ffn_in['w_down'], 'L0_ffn_amplitudes': _L0_ffn_in['amplitudes'], 'L0_ffn_expert_scale': _L0_ffn_in['expert_scale'], 'L0_ffn_shared_w_gate': _L0_ffn_in['shared_w_gate'], 'L0_ffn_shared_w_up': _L0_ffn_in['shared_w_up'], 'L0_ffn_shared_w_down': _L0_ffn_in['shared_w_down']}

def reference(x, ctx_2048, L0_ffn_w_router, L0_ffn_w_gate, L0_ffn_w_up, L0_ffn_w_down, L0_ffn_amplitudes, L0_ffn_expert_scale, L0_ffn_shared_w_gate, L0_ffn_shared_w_up, L0_ffn_shared_w_down):
    import jax
    import jax.numpy as jnp

    def _L0_xattn_ref(x, weight):
        import jax, jax.numpy as jnp
        import numpy as np
        FP8_MAX = 448.0
        ACT_EPS = 0.0001
        W_EPS = 1e-06
        BLK = 128

        def quant_dequant_act_1x128(x):
            E, M, K = x.shape
            xb = x.reshape(E, M, K // BLK, BLK)
            amax = jnp.max(jnp.abs(xb), axis=-1, keepdims=True)
            safe = jnp.maximum(amax, ACT_EPS)
            q = (xb * (FP8_MAX / safe)).astype(jnp.float8_e4m3fn)
            return (q.astype(jnp.float32) * (safe / FP8_MAX)).reshape(E, M, K)

        def quant_dequant_weight_128x128(w):
            E, N, K = w.shape
            wb = w.reshape(E, N // BLK, BLK, K // BLK, BLK)
            amax = jnp.max(jnp.abs(wb), axis=(2, 4), keepdims=True)
            safe = jnp.maximum(amax, W_EPS)
            q = (wb * (FP8_MAX / safe)).astype(jnp.float8_e4m3fn)
            return (q.astype(jnp.float32) * (safe / FP8_MAX)).reshape(E, N, K)
        xq = quant_dequant_act_1x128(x)
        wq = quant_dequant_weight_128x128(weight)
        return jnp.einsum('emk,enk->emn', xq, wq)

    def _L0_ffn_ref(x, w_router, w_gate, w_up, w_down, amplitudes, expert_scale, shared_w_gate, shared_w_up, shared_w_down):
        import jax, jax.numpy as jnp
        import numpy as np
        H = 512
        I = 256
        K = 8
        E = 128
        TOPK = 4
        EPS = 1e-08
        B, S, _ = x.shape
        T = B * S
        xt = x.reshape(T, H)
        probs = jax.nn.softmax(xt @ w_router, axis=-1)
        topk_p, topk_idx = jax.lax.top_k(probs, TOPK)
        topk_w = topk_p / (jnp.sum(topk_p, axis=-1, keepdims=True) + EPS)
        gate = (xt @ w_gate).reshape(T, K, I)
        up = (xt @ w_up).reshape(T, K, I)
        basis = jax.nn.silu(gate) * up
        p = amplitudes[..., 0] ** 2 + amplitudes[..., 1] ** 2
        mix = p / (jnp.sum(p, axis=-1, keepdims=True) + EPS)
        mix_sel = mix[topk_idx]
        mixed = jnp.einsum('tek,tki->tei', mix_sel, basis)
        down = jnp.einsum('tei,ih->teh', mixed, w_down)
        coeff = topk_w * expert_scale[topk_idx]
        out = jnp.einsum('teh,te->th', down, coeff)
        shared = jax.nn.silu(xt @ shared_w_gate) * (xt @ shared_w_up) @ shared_w_down
        out = out + shared
        return out.reshape(B, S, H)
    x = x + _L0_xattn_ref(_layernorm(x, axis=-1), ctx_2048)
    x = x + _L0_ffn_ref(_layernorm(x, axis=-1), L0_ffn_w_router, L0_ffn_w_gate, L0_ffn_w_up, L0_ffn_w_down, L0_ffn_amplitudes, L0_ffn_expert_scale, L0_ffn_shared_w_gate, L0_ffn_shared_w_up, L0_ffn_shared_w_down)
    return x

_drawn_inputs = setup_inputs


def setup_inputs(seed=0):
    import zlib

    import numpy as np

    out = dict(_drawn_inputs(seed))
    spreads = {'L0_ffn_expert_scale': (1.0, 0.6)}
    factors = {'L0_ffn_w_router': 8.0,
     'L0_ffn_w_gate': 4.639,
     'L0_ffn_w_up': 4.542,
     'L0_ffn_w_down': 4.53,
     'L0_ffn_amplitudes': 8.0,
     'L0_ffn_shared_w_gate': 2.759,
     'L0_ffn_shared_w_up': 2.702,
     'L0_ffn_shared_w_down': 2.705}
    for name, (base, spread) in spreads.items():
        noise = np.random.default_rng([zlib.crc32(name.encode()), seed]).standard_normal(out[name].shape)
        drawn = base * np.exp(spread * noise) if base else spread * noise
        out[name] = jnp.asarray(drawn.astype(out[name].dtype))
    for name, factor in factors.items():
        out[name] = (out[name] * factor).astype(out[name].dtype)
    return out
```

```python
from contextlib import ExitStack

import concourse.bass as bass
from concourse import mybir

ALU = mybir.AluOpType
ACT = mybir.ActivationFunctionType
AX = mybir.AxisListType
F32 = mybir.dt.float32
F16 = mybir.dt.float16
BF16 = mybir.dt.bfloat16
U32 = mybir.dt.uint32
I32 = mybir.dt.int32
ABSMAX = bass.bass_isa.ReduceOp.absmax

P = 128
EXPONENT = 0x7F800000
FP8_MAX = 448.0
FP8_TINY = 2.0 ** -6
ROUND = 1.5 * 2.0 ** 20
ACT_EPS = 1e-4
W_EPS = 1e-6
LN_EPS = 1e-5
TOP_EPS = 1e-8
LN_GAIN = 2.0 ** 10
TO_2_14 = 2.0 ** -14
SMALLEST = 1e-30


class Chain:

    def __init__(self, eng, sem, per_tile, t):
        self.eng, self.sem, self.per_tile, self.base, self.n = eng, sem, per_tile, per_tile * t, 0

    def did(self, instruction):
        instruction.then_inc(self.sem, 1)
        self.n += 1

    def sync(self, back=0):
        self.eng.wait_ge(self.sem, self.base + (self.n - back))

    def end(self):
        assert self.n == self.per_tile, (self.n, self.per_tile)


def settle(eng, passed):
    eng.sem_inc(passed, 1)


def wait_at(eng, sem, value):
    if not isinstance(value, int) or value > 0:
        eng.wait_ge(sem, value)


def build(nc, x, ctx, w_router, w_gate, w_up, w_down, amplitudes, expert_scale,
          s_gate, s_up, s_down, out):
    B, S, D = x.shape
    E = w_router.shape[1]
    I = w_down.shape[0]
    K = w_gate.shape[1] // I
    TOPK = 4
    KC = D // P
    NB = S // P
    TILES = B * NB
    CW = 512
    KPC = CW // I
    PAIRS = K // KPC
    IS = s_gate.shape[1]
    HW = I + IS
    HC = HW // P
    CHUNKS = 2 + 2 * (PAIRS + 1)
    DOWN = CHUNKS - 1
    assert IS == CW and D == CW and E == P and NB == 4
    STEPS = TILES // NB

    x_t = x.rearrange("b s d -> (b s) d")
    ctx_t = ctx.rearrange("b s d -> (b s) d")
    out_t = out.rearrange("b s d -> (b s) d")

    with ExitStack() as stack:
        def sb(name, shape, dt=F32):
            return stack.enter_context(nc.sbuf_tensor(name, shape, dt))

        def sem(name):
            return stack.enter_context(nc.semaphore(name))

        stage = sb("stage", [P, 3, HC * CW])
        wr = [sb(f"router_{h}", [P, KC, E], F16) for h in ("hi", "lo")]
        wgu = [sb(f"gate_up_{h}", [P, 2 * (PAIRS + 1), KC, CW], F16) for h in ("hi", "lo")]
        wd = [sb(f"down_{h}", [P, HC, D], F16) for h in ("hi", "lo")]
        w_max = sb("w_max", [P, CHUNKS])
        w_all = sb("w_all", [P, CHUNKS])
        w_tmp = sb("w_tmp", [P, CHUNKS])
        w_unscale = sb("w_unscale", [P, CHUNKS])
        w_scale = sb("w_scale", [P, CHUNKS])
        w_back = sb("w_back", [P, CHUNKS])
        ident32 = sb("ident32", [P, P])
        ident16 = sb("ident16", [P, P], F16)
        identb = sb("identb", [P, P], BF16)
        iota_i = sb("iota_i", [P, P], I32)
        iota = sb("iota", [P, P])
        minus_half = sb("minus_half", [P, 1])
        amp = sb("amp", [P, K, 2])
        amp_sq = sb("amp_sq", [P, K, 2])
        power = sb("power", [P, K])
        power_sum = sb("power_sum", [P, 2])
        escale = sb("escale", [P, 1])
        mix = sb("mix", [P, K])

        ctx_in = sb("ctx_in", [P, NB, D])
        ctx_max = sb("ctx_max", [P, KC])
        ctx_all = sb("ctx_all", [P, KC])
        ctx_safe = sb("ctx_safe", [P, KC])
        ctx_rec = sb("ctx_rec", [P, KC])
        ctx_mul = sb("ctx_mul", [P, KC])
        round_v = sb("round_v", [P, D])
        round_m = sb("round_m", [P, D])
        ctx_q = sb("ctx_q", [P, D], BF16)
        ctx_qT = sb("ctx_qT", [P, B, KC, S], BF16)
        ctx_scale = sb("ctx_scale", [P, TILES, KC])

        x_in = sb("x_in", [P, 2, D])
        stat = sb("stat", [P, 6])
        mv = sb("mv", [P, 2])
        var = sb("var", [P, 1])
        rstd = sb("rstd", [P, 1])
        y = sb("y", [P, D])
        x_max = sb("x_max", [P, KC])
        x_safe = sb("x_safe", [P, KC])
        x_rec = sb("x_rec", [P, KC])
        x_mul = sb("x_mul", [P, KC])
        x_scale = sb("x_scale", [P, KC])
        x_q = sb("x_q", [P, D], BF16)
        x_qT = sb("x_qT", [P, KC, P], BF16)
        both_scale = sb("both_scale", [P, NB, KC])
        x2 = sb("x2", [P, 2, D])
        stat2 = sb("stat2", [P, 6])
        mv2 = sb("mv2", [P, 2])
        var2 = sb("var2", [P, 1])
        rstd2 = sb("rstd2", [P, 1])
        gain2 = sb("gain2", [P, 1])
        y2 = sb("y2", [P, D])
        z = [sb(f"z_{h}", [P, D], F16) for h in ("hi", "lo")]
        zT = [sb(f"zT_{h}", [P, 2, KC, P], F16) for h in ("hi", "lo")]

        logit = sb("logit", [P, E])
        top8 = sb("top8", [P, 8])
        idx8 = sb("idx8", [P, 8], U32)
        idx = sb("idx", [P, TOPK])
        neg_max = sb("neg_max", [P, 1])
        prob = sb("prob", [P, E])
        prob_sum = sb("prob_sum", [P, 1])
        picked = [sb(f"picked{i}", [P, E]) for i in range(2)]
        weight = sb("weight", [P, E])
        weight_sum = sb("weight_sum", [P, 1])
        denom = sb("denom", [P, 1])
        inv_denom = sb("inv_denom", [P, 1])
        weightT = sb("weightT", [P, P])
        coef = sb("coef", [P, K])

        silu = sb("silu", [P, 2, CW])
        basis = y
        hid = sb("hid", [P, 2, HW])
        hid_max = sb("hid_max", [P, 1])
        hid_tmp = sb("hid_tmp", [P, 1])
        hid_unscale = sb("hid_unscale", [P, 1])
        hid_scale = sb("hid_scale", [P, 1])
        out_scale = sb("out_scale", [P, 1])
        hs = [sb(f"hs_{h}", [P, HW], F16) for h in ("hi", "lo")]
        hT = [sb(f"hT_{h}", [P, HC, P], F16) for h in ("hi", "lo")]
        y_out = sb("y_out", [P, 2, D])

        def bank(name):
            return stack.enter_context(nc.psum_tensor(name, [P, 512], F32))

        gate_ps = [bank("gate0"), bank("gate1")]
        up_ps = [bank("up0"), bank("up1")]
        turn_ps = [bank("turn0"), bank("turn1")]
        even_ps, odd_ps = bank("even"), bank("odd")
        turned = [t[:].bitcast(F16) for t in turn_ps]

        stage_in = [sem(f"stage_in{i}") for i in range(3)]
        small_in = sem("small_in")
        ctx_loaded = [sem(f"ctx_loaded{i}") for i in range(NB)]
        x_loaded = [sem(f"x_loaded{i}") for i in range(2)]
        made = sem("made")
        consts = sem("consts")
        passed_dve, passed_pool = sem("passed_dve"), sem("passed_pool")
        mix_step = sem("mix_step")
        w_maxed, w_reduced = sem("w_maxed"), sem("w_reduced")
        w_step, w_hi_done, w_ready = sem("w_step"), sem("w_hi_done"), sem("w_ready")
        ctx_maxed, ctx_reduced = sem("ctx_maxed"), sem("ctx_reduced")
        ctx_step, ctx_turned, ctx_kept = sem("ctx_step"), sem("ctx_turned"), sem("ctx_kept")
        stat_step, rstd_done = sem("stat_step"), sem("rstd_done")
        xq_step, x_turned, x_kept = sem("xq_step"), sem("x_turned"), sem("x_kept")
        att_full, att_step, both_done = sem("att_full"), sem("att_step"), sem("both_done")
        ln_step, rstd2_done = sem("ln_step"), sem("rstd2_done")
        z_hi_done, z_turned, z_kept = sem("z_hi_done"), sem("z_turned"), sem("z_kept")
        logit_full, top_step, exp_done = sem("logit_full"), sem("top_step"), sem("exp_done")
        weight_turned, weightT_kept = sem("weight_turned"), sem("weightT_kept")
        coef_full, coef_done = sem("coef_full"), sem("coef_done")
        gate_full, up_full, silu_done = sem("gate_full"), sem("up_full"), sem("silu_done")
        pair_read, mix_acc = sem("pair_read"), sem("mix_acc")
        hid_step, h_hi_done = sem("hid_step"), sem("h_hi_done")
        h_turned, h_kept = sem("h_turned"), sem("h_kept")
        down_full, down_read = sem("down_full"), sem("down_read")
        stored = [sem(f"stored{i}") for i in range(2)]

        CTX_STEPS, STAT_STEPS, XQ_STEPS, ATT_STEPS, LN_STEPS = 9, 3, 10, 16, 6
        TOP_STEPS, HID_STEPS, W_STEPS, MIX_STEPS, MIX_ACC = 12, 6, 4, 4, 8

        def use(t, p):
            return (PAIRS + 1) * t + (1 + p)

        def parity(j, p):
            return (j + 1 + p) % 2

        def chunk(p):
            return 1 + 2 * (p + 1)

        def by_batch(eng, step):
            with eng.Fori(0, STEPS - 1) as b:
                for j in range(NB):
                    step(b, j, False)
            for j in range(NB):
                step(STEPS - 1, j, True)

        def w_part(h, n):
            if n == 0:
                return wr[h][:].rearrange("p c w -> p (c w)")
            if n == DOWN:
                return wd[h][:].rearrange("p c w -> p (c w)")
            return wgu[h][:, n - 1].rearrange("p c w -> p (c w)")

        def w_staged(n):
            width = KC * E if n == 0 else HC * D if n == DOWN else KC * CW
            return stage[:, n % 3, 0:width]

        block = stack.enter_context(nc.Block())

        @block.sync
        def _(sp):
            def load_ctx(b, j):
                if not isinstance(b, int) or b > 0:
                    sp.wait_ge(ctx_step, CTX_STEPS * (b * NB + j - NB) + 5)
                sp.dma_start(ctx_in[:, j, :], ctx_t[bass.ds((b * NB + j) * P, P), :]
                             ).then_inc(ctx_loaded[j], 16)

            def load_x(t, j):
                if not isinstance(t, int) or t >= 2:
                    sp.wait_ge(att_step, ATT_STEPS * (t - 2) + NB)
                sp.dma_start(x_in[:, j % 2, :], x_t[bass.ds(t * P, P), :]).then_inc(x_loaded[j % 2], 16)

            def load_chunk(n):
                if n >= 3:
                    sp.wait_ge(w_ready, n - 2)
                slot = stage[:, n % 3, :]

                def put(dst0, src):
                    kc = src.shape[0] // P
                    w = src.shape[1]
                    sp.dma_start(slot[:, dst0:dst0 + kc * w].rearrange("p (c w) -> p c w", c=kc),
                                 src.rearrange("(c p) w -> p c w", p=P)).then_inc(stage_in[n % 3], 16)

                if n == 0:
                    put(0, w_router)
                elif n == DOWN:
                    put(0, w_down)
                    put(I // P * D, s_down)
                else:
                    src = (s_gate, s_up) if n <= 2 else (w_gate, w_up)
                    col = 0 if n <= 2 else (n - 3) // 2 * CW
                    put(0, src[(n - 1) % 2][:, col:col + CW])

            load_ctx(0, 0)
            load_x(0, 0)
            for j in range(1, NB):
                load_ctx(0, j)
            load_chunk(0)
            sp.dma_start(amp[:], amplitudes).then_inc(small_in, 16)
            sp.dma_start(escale[:], expert_scale.rearrange("(e o) -> e o", o=1)).then_inc(small_in, 16)
            load_chunk(1)
            load_chunk(2)
            load_x(1, 1)
            for n in range(3, CHUNKS):
                load_chunk(n)

            def step(b, j, last):
                if not last:
                    load_ctx(b + 1, j)
                if not last or j + 2 < NB:
                    load_x(b * NB + (j + 2), j)

            by_batch(sp, step)

        @block.gpsimd
        def _(pool):
            nc.gpsimd.memset(minus_half[:], -0.5).then_inc(made, 1)
            nc.gpsimd.iota(iota_i[:], [[1, P]], base=0, channel_multiplier=0).then_inc(made, 1)
            nc.gpsimd.memset(ident32[:], 0.0).then_inc(made, 1)
            pool.wait_ge(made, 3)
            nc.gpsimd.affine_select(out=ident32[:], in_=ident32[:], compare_op=ALU.not_equal, fill=1.0,
                                    base=0, pattern=[[-1, P]], channel_multiplier=1).then_inc(made, 1)

            def reduce_ctx(c):
                pool.wait_ge(ctx_maxed, c + 1)
                settle(pool, passed_pool)
                nc.gpsimd.partition_all_reduce(ctx_all[:], ctx_max[:], P, ABSMAX).then_inc(ctx_reduced, 1)

            def reduce_w(n):
                pool.wait_ge(w_maxed, n + 1)
                nc.gpsimd.partition_all_reduce(w_all[:, n:n + 1], w_max[:, n:n + 1], P, ABSMAX
                                               ).then_inc(w_reduced, 1)

            def rstd_of(t):
                pool.wait_ge(stat_step, STAT_STEPS * (t + 1))
                nc.gpsimd.tensor_tensor(rstd[:], var[:], minus_half[:], ALU.pow).then_inc(rstd_done, 1)

            def rstd2_of(t):
                pool.wait_ge(ln_step, LN_STEPS * t + 3)
                nc.gpsimd.tensor_tensor(rstd2[:], var2[:], minus_half[:], ALU.pow).then_inc(rstd2_done, 1)

            reduce_ctx(0)
            rstd_of(0)
            for c in range(1, NB):
                reduce_ctx(c)
            reduce_w(0)
            reduce_w(1)
            rstd2_of(0)
            for n in range(2, CHUNKS):
                reduce_w(n)

            def step(b, j, last):
                t = b * NB + (j + 1)
                if not last:
                    reduce_ctx((b + 1) * NB + j)
                if not last or j + 1 < NB:
                    rstd_of(t)
                    rstd2_of(t)

            by_batch(pool, step)

        @block.scalar
        def _(act):
            def split_w(n):
                act.wait_ge(w_step, W_STEPS * (n + 1))
                dst = w_part(0, n)
                nc.scalar.activation(dst, w_staged(n), ACT.Copy, scale=w_scale[:, n:n + 1]
                                     ).then_inc(w_hi_done, 1)

            def keep_ctx(b, j):
                act.wait_ge(ctx_turned, b * NB + (j + 1))
                nc.scalar.copy(ctx_qT[:, b, :, j * P:(j + 1) * P] if isinstance(b, int) else
                               ctx_qT[:, bass.ds(b, 1), :, j * P:(j + 1) * P].rearrange("p o c n -> p (o c) n"),
                               turned[0].bitcast(BF16)[:, 0:KC * P].rearrange("p (c n) -> p c n", c=KC)
                               ).then_inc(ctx_kept, 1)

            def keep_x(t):
                act.wait_ge(x_turned, t + 1)
                wait_at(act, att_full, KC * t)
                nc.scalar.copy(x_qT[:].rearrange("p c n -> p (c n)"), turned[1].bitcast(BF16)[:, 0:KC * P]
                               ).then_inc(x_kept, 1)

            def z_hi(t):
                act.wait_ge(ln_step, LN_STEPS * t + 5)
                wait_at(act, z_turned, 2 * t)
                nc.scalar.copy(z[0][:], y2[:]).then_inc(z_hi_done, 1)

            def keep_z(t, j):
                for h in range(2):
                    act.wait_ge(z_turned, 2 * t + (h + 1))
                    nc.scalar.copy(zT[h][:, j % 2].rearrange("p c n -> p (c n)"), turned[h][:, 0:KC * P]
                                   ).then_inc(z_kept, 1)

            def exps(t):
                act.wait_ge(top_step, TOP_STEPS * t + 5)
                nc.scalar.activation(prob[:], logit[:], ACT.Exp, bias=neg_max[:], accum_out=prob_sum[:]
                                     ).then_inc(exp_done, 1)

            def silus(t, j, p):
                k, par = use(t, p), parity(j, p)
                act.wait_ge(gate_full, k + 1)
                wait_at(act, pair_read, k)
                n = chunk(p)
                if isinstance(t, int) and t == 0:
                    act.wait_ge(w_step, W_STEPS * (n + 1))
                nc.scalar.activation(silu[:, par, :], gate_ps[par][:], ACT.Silu, scale=w_back[:, n:n + 1]
                                     ).then_inc(silu_done, 1)

            def h_hi(s, j):
                act.wait_ge(hid_step, HID_STEPS * s + 4)
                nc.scalar.activation(hs[0][:], hid[:, j % 2, :], ACT.Copy, scale=hid_scale[:]
                                     ).then_inc(h_hi_done, 1)

            def keep_h(s):
                for h in range(2):
                    act.wait_ge(h_turned, 2 * s + (h + 1))
                    nc.scalar.copy(hT[h][:].rearrange("p c n -> p (c n)"), turned[h][:, 0:HW]
                                   ).then_inc(h_kept, 1)

            def store(s, j):
                act.wait_ge(down_read, s + 2)
                act.dma_start(out_t[bass.ds(s * P, P), :], y_out[:, j % 2, :]).then_inc(stored[j % 2], 16)

            act.sem_inc(stored[0], 16)
            act.sem_inc(stored[1], 16)
            for c in range(NB):
                keep_ctx(0, c)
            keep_x(0)
            split_w(0)
            split_w(1)
            z_hi(0)
            keep_z(0, 0)
            split_w(2)
            exps(0)
            silus(0, 0, -1)
            for n in range(3, CHUNKS):
                split_w(n)

            def step(b, j, last):
                s, t = b * NB + j, b * NB + (j + 1)
                front = not last or j + 1 < NB
                silus(s, j, 0)
                silus(s, j, 1)
                if not last:
                    keep_ctx(b + 1, j)
                if front:
                    keep_x(t)
                silus(s, j, 2)
                if front:
                    z_hi(t)
                silus(s, j, 3)
                if front:
                    keep_z(t, j + 1)
                h_hi(s, j)
                if front:
                    exps(t)
                    silus(t, j + 1, -1)
                keep_h(s)
                store(s, j)

            by_batch(act, step)
            act.wait_ge(stored[0], 16 * (TILES // 2) + 16)
            act.wait_ge(stored[1], 16 * (TILES // 2) + 16)

        @block.tensor
        def _(pe):
            HI_LO = ((0, 0), (0, 1), (1, 0))

            def turn_ctx(c):
                pe.wait_ge(ctx_step, CTX_STEPS * (c + 1))
                wait_at(pe, ctx_kept, c)
                ps = turned[0].bitcast(BF16)
                for kc in range(KC):
                    mm = nc.tensor.transpose(ps[:, kc * P:(kc + 1) * P], ctx_q[:, kc * P:(kc + 1) * P], identb[:])
                mm.then_inc(ctx_turned, 1)

            def turn_x(t):
                pe.wait_ge(xq_step, XQ_STEPS * (t + 1))
                ps = turned[1].bitcast(BF16)
                for kc in range(KC):
                    mm = nc.tensor.transpose(ps[:, kc * P:(kc + 1) * P], x_q[:, kc * P:(kc + 1) * P], identb[:])
                mm.then_inc(x_turned, 1)

            def attend(t, b, kc):
                if kc == 0:
                    pe.wait_ge(x_kept, t + 1)
                    pe.wait_ge(ctx_kept, (b + 1) * NB)
                    wait_at(pe, down_read, t)
                elif kc == 1:
                    wait_at(pe, coef_done, t)
                else:
                    pe.wait_ge(att_step, ATT_STEPS * t + (kc - 1) * NB)
                ps = (even_ps, odd_ps)[kc % 2]
                rhs = (ctx_qT[:, b, kc, :] if isinstance(b, int) else
                       ctx_qT[:, bass.ds(b, 1), kc, :].rearrange("p o n -> p (o n)"))
                nc.tensor.matmul(ps[:], x_qT[:, kc, :], rhs, start=True, stop=True).then_inc(att_full, 1)

            def turn_z(t):
                for h in range(2):
                    if h == 0:
                        pe.wait_ge(z_hi_done, t + 1)
                        pe.wait_ge(ctx_kept, min(t + NB, TILES) if isinstance(t, int) else t + NB)
                    else:
                        pe.wait_ge(ln_step, LN_STEPS * (t + 1))
                    for kc in range(KC):
                        mm = nc.tensor.transpose(turned[h][:, kc * P:(kc + 1) * P],
                                                 z[h][:, kc * P:(kc + 1) * P], ident16[:])
                    mm.then_inc(z_turned, 1)

            def route(t, j):
                pe.wait_ge(z_kept, 2 * (t + 1))
                pe.wait_ge(w_ready, 1)
                pe.wait_ge(att_step, ATT_STEPS * (t + 1))
                n = 0
                for kc in range(KC):
                    for a, w in HI_LO:
                        mm = nc.tensor.matmul(odd_ps[:, 0:E], zT[a][:, j % 2, kc, :], wr[w][:, kc, :],
                                              start=(n == 0), stop=(n == 3 * KC - 1))
                        n += 1
                mm.then_inc(logit_full, 1)

            def pair(t, j, p, between={}):
                k, par, n = use(t, p), parity(j, p), chunk(p)
                wait_at(pe, pair_read, k)
                for i, (ps, full) in enumerate(((gate_ps[par], gate_full), (up_ps[par], up_full))):
                    pe.wait_ge(w_ready, n + i + 1)
                    m = 0
                    for kc in range(KC):
                        if kc % 2 == 0 and 2 * i + kc // 2 in between:
                            between[2 * i + kc // 2]()
                        for a, w in HI_LO:
                            mm = nc.tensor.matmul(ps[:], zT[a][:, j % 2, kc, :], wgu[w][:, n - 1 + i, kc, :],
                                                  start=(m == 0), stop=(m == 3 * KC - 1))
                            m += 1
                    mm.then_inc(full, 1)

            def turn_h(s):
                for h in range(2):
                    if h == 0:
                        pe.wait_ge(h_hi_done, s + 1)
                    else:
                        pe.wait_ge(hid_step, HID_STEPS * (s + 1))
                    for hc in range(HC):
                        mm = nc.tensor.transpose(turned[h][:, hc * P:(hc + 1) * P],
                                                 hs[h][:, hc * P:(hc + 1) * P], ident16[:])
                    mm.then_inc(h_turned, 1)

            def turn_weight(t):
                pe.wait_ge(top_step, TOP_STEPS * (t + 1) - 2)
                nc.tensor.transpose(odd_ps[:, 0:P], weight[:], ident32[:]).then_inc(weight_turned, 1)

            def coefs(t):
                pe.wait_ge(weightT_kept, t + 1)
                if isinstance(t, int) and t == 0:
                    pe.wait_ge(mix_step, MIX_STEPS)
                nc.tensor.matmul(odd_ps[:, 0:K], weightT[:], mix[:], start=True, stop=True
                                 ).then_inc(coef_full, 1)

            def down(s, between={}):
                pe.wait_ge(w_ready, CHUNKS)
                n = 0
                for a, w in ((0, 0), (0, 1), (1, 0)):
                    if (a, w) in between:
                        between[(a, w)]()
                    if w == 0:
                        pe.wait_ge(h_kept, 2 * s + (a + 1))
                    for hc in range(HC):
                        mm = nc.tensor.matmul(even_ps[:], hT[a][:, hc, :], wd[w][:, hc, :],
                                              start=(n == 0), stop=(n == 3 * HC - 1))
                        n += 1
                mm.then_inc(down_full, 1)

            pe.wait_ge(consts, 3)
            for c in range(NB):
                turn_ctx(c)
            turn_x(0)
            for kc in range(KC):
                attend(0, 0, kc)
            turn_z(0)
            route(0, 0)
            pair(0, 0, -1)
            turn_weight(0)
            coefs(0)

            def step(b, j, last):
                s, t = b * NB + j, b * NB + (j + 1)
                bt = b + 1 if j + 1 == NB else b
                front = not last or j + 1 < NB
                pair(s, j, 0)
                pair(s, j, 1, {} if last else {3: lambda: turn_ctx((b + 1) * NB + j)})

                def first_half():
                    attend(t, bt, 0)
                    attend(t, bt, 1)

                def second_half():
                    attend(t, bt, 2)
                    attend(t, bt, 3)

                pair(s, j, 2, {0: lambda: turn_x(t), 1: first_half, 3: second_half} if front else {})
                pair(s, j, 3, {3: lambda: turn_z(t)} if front else {})
                if front:
                    route(t, j + 1)
                    pair(t, j + 1, -1, {3: lambda: turn_h(s)})
                    pe.wait_ge(att_step, ATT_STEPS * (t + 1))
                    down(s, {(0, 1): lambda: turn_weight(t), (1, 0): lambda: coefs(t)})
                else:
                    turn_h(s)
                    down(s)

            by_batch(pe, step)

        @block.vector
        def _(dve):
            dve.sem_inc(pair_read, 1)
            dve.sem_inc(down_read, 1)

            def quantise(ch, src, mul, q, before_q, scratch_free):
                v, m = round_v, round_m
                scratch_free()
                c4 = lambda a: a.rearrange("p (c n) -> p c n", c=KC)
                ch.did(nc.vector.tensor_tensor(c4(v[:]), c4(src), mul[:].unsqueeze(2).to_broadcast([P, KC, P]),
                                               ALU.mult))
                ch.sync()
                ch.did(nc.vector.tensor_scalar(m[:].bitcast(U32), v[:].bitcast(U32), EXPONENT, None,
                                               ALU.bitwise_and))
                ch.sync()
                ch.did(nc.vector.tensor_scalar(m[:], m[:], FP8_TINY, ROUND, ALU.max, ALU.mult))
                ch.sync()
                ch.did(nc.vector.tensor_tensor(v[:], v[:], m[:], ALU.add))
                ch.sync()
                before_q()
                ch.did(nc.vector.tensor_tensor(q[:], v[:], m[:], ALU.subtract))

            def max_ctx(b, j):
                dve.wait_ge(ctx_loaded[j], 16 * (b + 1))
                nc.vector.tensor_reduce(ctx_max[:], ctx_in[:, j, :].rearrange("p (c n) -> p c n", c=KC),
                                        AX.X, ALU.max, apply_absolute_value=True).then_inc(ctx_maxed, 1)

            def quant_ctx(b, j, scratch_free):
                c = b * NB + j
                ch = Chain(dve, ctx_step, CTX_STEPS, c)
                dve.wait_ge(ctx_reduced, c + 1)
                ch.did(nc.vector.tensor_scalar(ctx_safe[:], ctx_all[:], W_EPS, None, ALU.max))
                ch.sync()
                ch.did(nc.vector.reciprocal(ctx_rec[:], ctx_safe[:]))
                ch.did(nc.vector.tensor_scalar(ctx_scale[:, bass.ds(c, 1), :].rearrange("p o c -> p (o c)"),
                                               ctx_safe[:], 1.0 / FP8_MAX, None, ALU.mult))
                ch.sync(1)
                ch.did(nc.vector.tensor_scalar(ctx_mul[:], ctx_rec[:], FP8_MAX, None, ALU.mult))
                ch.sync()
                quantise(ch, ctx_in[:, j, :], ctx_mul, ctx_q,
                         lambda: wait_at(dve, ctx_turned, c),
                         scratch_free)
                ch.end()

            def stats(t, j):
                ch = Chain(dve, stat_step, STAT_STEPS, t)
                dve.wait_ge(x_loaded[j % 2], 16 * ((t - j % 2) // 2 + 1) if isinstance(t, int) else
                            (t - j % 2) * 8 + 16)
                ch.did(nc.vector.bn_stats(stat[:], x_in[:, j % 2, :]))
                ch.sync()
                settle(dve, passed_dve)
                ch.did(nc.vector.bn_aggr(mv[:], stat[:]))
                ch.sync()
                ch.did(nc.vector.tensor_scalar(var[:], mv[:, 1:2], LN_EPS, None, ALU.add))
                ch.end()

            def quant_x(t, j, scratch_free):
                ch = Chain(dve, xq_step, XQ_STEPS, t)
                wait_at(dve, mix_acc, MIX_ACC * (t - 1) + KPC if not isinstance(t, int) or t else 0)
                dve.wait_ge(rstd_done, t + 1)
                ch.did(nc.vector.tensor_scalar(y[:], x_in[:, j % 2, :], mv[:, 0:1], rstd[:],
                                               ALU.subtract, ALU.mult))
                ch.sync()
                ch.did(nc.vector.tensor_reduce(x_max[:], y[:].rearrange("p (c n) -> p c n", c=KC),
                                               AX.X, ALU.max, apply_absolute_value=True))
                ch.sync()
                ch.did(nc.vector.tensor_scalar(x_safe[:], x_max[:], ACT_EPS, None, ALU.max))
                ch.sync()
                ch.did(nc.vector.reciprocal(x_rec[:], x_safe[:]))
                ch.sync()
                ch.did(nc.vector.tensor_scalar(x_mul[:], x_rec[:], FP8_MAX, None, ALU.mult))
                ch.sync()
                quantise(ch, y[:], x_mul, x_q, lambda: wait_at(dve, x_turned, t), scratch_free)
                ch.end()

            def attention(t, j, b):
                dve.wait_ge(xq_step, XQ_STEPS * t + 3)
                dve.wait_ge(ctx_step, CTX_STEPS * (b + 1) * NB)
                nc.vector.tensor_scalar(x_scale[:], x_safe[:], 1.0 / FP8_MAX, None, ALU.mult
                                        ).then_inc(both_done, 1)
                dve.wait_ge(both_done, 2 * t + 1)
                nc.vector.tensor_tensor(both_scale[:], ctx_scale[:, bass.ds(b * NB, NB), :],
                                        x_scale[:].unsqueeze(1).to_broadcast([P, NB, KC]), ALU.mult
                                        ).then_inc(both_done, 1)
                dve.wait_ge(both_done, 2 * t + 2)
                ch = Chain(dve, att_step, ATT_STEPS, t)
                for kc in range(KC):
                    dve.wait_ge(att_full, KC * t + (kc + 1))
                    ps = (even_ps, odd_ps)[kc % 2]
                    for nb in range(NB):
                        cols = slice(nb * P, (nb + 1) * P)
                        prev = x_in[:, j % 2, cols] if kc == 0 else x2[:, j % 2, cols]
                        if kc > 0:
                            ch.sync(NB - 1)
                        ch.did(nc.vector.scalar_tensor_tensor(x2[:, j % 2, cols], ps[:, cols],
                                                              both_scale[:, nb, kc:kc + 1], prev,
                                                              ALU.mult, ALU.add))
                ch.end()

            def norm2(t, j):
                ch = Chain(dve, ln_step, LN_STEPS, t)
                dve.wait_ge(att_step, ATT_STEPS * (t + 1))
                ch.did(nc.vector.bn_stats(stat2[:], x2[:, j % 2, :]))
                ch.sync()
                settle(dve, passed_dve)
                ch.did(nc.vector.bn_aggr(mv2[:], stat2[:]))
                ch.sync()
                ch.did(nc.vector.tensor_scalar(var2[:], mv2[:, 1:2], LN_EPS, None, ALU.add))
                dve.wait_ge(rstd2_done, t + 1)
                ch.did(nc.vector.tensor_scalar(gain2[:], rstd2[:], LN_GAIN, None, ALU.mult))
                ch.sync()
                ch.did(nc.vector.tensor_scalar(y2[:], x2[:, j % 2, :], mv2[:, 0:1], gain2[:],
                                               ALU.subtract, ALU.mult))
                dve.wait_ge(z_hi_done, t + 1)
                wait_at(dve, z_turned, 2 * t)
                ch.did(nc.vector.tensor_tensor(z[1][:], y2[:], z[0][:], ALU.subtract))
                ch.end()

            def top(t):
                ch = Chain(dve, top_step, TOP_STEPS, t)
                dve.wait_ge(logit_full, t + 1)
                ch.did(nc.vector.tensor_scalar(logit[:], odd_ps[:, 0:E], w_back[:, 0:1], None, ALU.mult))
                ch.sync()
                settle(dve, passed_dve)
                ch.did(nc.vector.max(top8[:], logit[:]))
                ch.sync()
                settle(dve, passed_dve)
                ch.did(nc.vector.max_index(idx8[:], top8[:], logit[:]))
                ch.sync()
                ch.did(nc.vector.tensor_copy(idx[:], idx8[:, 0:TOPK]))
                ch.did(nc.vector.tensor_scalar(neg_max[:], top8[:, 0:1], -1.0, None, ALU.mult))
                ch.sync(1)
                ch.did(nc.vector.tensor_scalar(picked[0][:], iota[:], idx[:, 0:1], None, ALU.is_equal))
                for i in range(1, TOPK):
                    ch.sync()
                    ch.did(nc.vector.scalar_tensor_tensor(picked[i % 2][:], iota[:], idx[:, i:i + 1],
                                                          picked[(i - 1) % 2][:], ALU.is_equal, ALU.add))
                ch.sync()
                dve.wait_ge(exp_done, t + 1)
                ch.did(nc.vector.scalar_tensor_tensor(weight[:], picked[(TOPK - 1) % 2][:], 1.0, prob[:],
                                                      ALU.mult, ALU.mult, accum_out=weight_sum[:]))
                ch.sync()
                ch.did(nc.vector.scalar_tensor_tensor(denom[:], prob_sum[:], TOP_EPS, weight_sum[:],
                                                      ALU.mult, ALU.add))
                ch.sync()
                ch.did(nc.vector.reciprocal(inv_denom[:], denom[:]))
                ch.end()

            def coefficients(t):
                dve.wait_ge(weight_turned, t + 1)
                nc.vector.tensor_copy(weightT[:], odd_ps[:, 0:P]).then_inc(weightT_kept, 1)
                dve.wait_ge(coef_full, t + 1)
                dve.wait_ge(top_step, TOP_STEPS * (t + 1))
                nc.vector.tensor_scalar(coef[:], odd_ps[:, 0:K], inv_denom[:], None, ALU.mult
                                        ).then_inc(coef_done, 1)

            def combine(t, j, p, front=False):
                k, par, n = use(t, p), parity(j, p), chunk(p) + 1
                dve.wait_ge(up_full, k + 1)
                dve.wait_ge(silu_done, k + 1)
                dst = hid[:, j % 2, I:HW] if p < 0 else basis[:]
                if p > 0:
                    dve.wait_ge(mix_acc, MIX_ACC * t + KPC * p)
                if p == 1 and front:
                    dve.wait_ge(xq_step, XQ_STEPS * (t + 2))
                nc.vector.scalar_tensor_tensor(dst, up_ps[par][:], w_back[:, n:n + 1], silu[:, par, :],
                                               ALU.mult, ALU.mult).then_inc(pair_read, 1)
                if p < 0:
                    return
                dve.wait_ge(pair_read, k + 2)
                dve.wait_ge(coef_done, t + 1)
                mixed = hid[:, j % 2, 0:I]
                for i in range(KPC):
                    kk = p * KPC + i
                    part = basis[:, i * I:(i + 1) * I]
                    if kk == 0:
                        ins = nc.vector.tensor_scalar(mixed, part, coef[:, 0:1], None, ALU.mult)
                    else:
                        dve.wait_ge(mix_acc, MIX_ACC * t + kk)
                        ins = nc.vector.scalar_tensor_tensor(mixed, part, coef[:, kk:kk + 1], mixed,
                                                             ALU.mult, ALU.add)
                    ins.then_inc(mix_acc, 1)

            def split_h(s, j):
                ch = Chain(dve, hid_step, HID_STEPS, s)
                dve.wait_ge(mix_acc, MIX_ACC * (s + 1))
                dve.wait_ge(pair_read, use(s, 3) + 2)
                ch.did(nc.vector.tensor_reduce(hid_max[:], hid[:, j % 2, :], AX.X, ALU.max,
                                               apply_absolute_value=True))
                ch.sync()
                ch.did(nc.vector.tensor_scalar(hid_tmp[:], hid_max[:], SMALLEST, TO_2_14, ALU.max, ALU.mult))
                ch.sync()
                ch.did(nc.vector.tensor_scalar(hid_unscale[:].bitcast(U32), hid_tmp[:].bitcast(U32),
                                               EXPONENT, None, ALU.bitwise_and))
                ch.sync()
                ch.did(nc.vector.reciprocal(hid_scale[:], hid_unscale[:]))
                ch.did(nc.vector.tensor_tensor(out_scale[:], hid_unscale[:], w_unscale[:, DOWN:DOWN + 1], ALU.mult))
                dve.wait_ge(h_hi_done, s + 1)
                ch.did(nc.vector.scalar_tensor_tensor(hs[1][:], hid[:, j % 2, :], hid_scale[:], hs[0][:],
                                                      ALU.mult, ALU.subtract))
                ch.end()

            def finish(s, j):
                dve.wait_ge(down_full, s + 1)
                dve.wait_ge(stored[j % 2], (s - j % 2) * 8 + 16)
                nc.vector.scalar_tensor_tensor(y_out[:, j % 2, :], even_ps[:], out_scale[:], x2[:, j % 2, :],
                                               ALU.mult, ALU.add).then_inc(down_read, 1)

            def max_w(n):
                dve.wait_ge(stage_in[n % 3], 16 * (n // 3 + 1) + (16 if n == DOWN else 0))
                nc.vector.tensor_reduce(w_max[:, n:n + 1], w_staged(n), AX.X, ALU.max,
                                        apply_absolute_value=True).then_inc(w_maxed, 1)

            def scale_w(n):
                ch = Chain(dve, w_step, W_STEPS, n)
                one = slice(n, n + 1)
                dve.wait_ge(w_reduced, n + 1)
                ch.did(nc.vector.tensor_scalar(w_tmp[:, one], w_all[:, one], SMALLEST, TO_2_14,
                                               ALU.max, ALU.mult))
                ch.sync()
                ch.did(nc.vector.tensor_scalar(w_unscale[:, one].bitcast(U32), w_tmp[:, one].bitcast(U32),
                                               EXPONENT, None, ALU.bitwise_and))
                ch.sync()
                ch.did(nc.vector.reciprocal(w_scale[:, one], w_unscale[:, one]))
                ch.did(nc.vector.tensor_scalar(w_back[:, one], w_unscale[:, one], 1.0 / LN_GAIN, None, ALU.mult))
                ch.end()

            def lo_w(n):
                dve.wait_ge(w_hi_done, n + 1)
                dve.wait_ge(w_step, W_STEPS * (n + 1))
                nc.vector.scalar_tensor_tensor(w_part(1, n), w_staged(n), w_scale[:, n:n + 1], w_part(0, n),
                                               ALU.mult, ALU.subtract).then_inc(w_ready, 1)

            def mixes():
                ch = Chain(dve, mix_step, MIX_STEPS, 0)
                dve.wait_ge(small_in, 32)
                nc.vector.tensor_tensor(amp_sq[:], amp[:], amp[:], ALU.mult).then_inc(mix_step, 1)
                ch.n += 1
                ch.sync()
                ch.did(nc.vector.tensor_tensor(power[:], amp_sq[:, :, 0], amp_sq[:, :, 1], ALU.add))
                ch.sync()
                ch.did(nc.vector.tensor_reduce(power_sum[:, 0:1], power[:], AX.X, ALU.add))
                ch.sync()
                nc.vector.tensor_scalar(power_sum[:, 0:1], power_sum[:, 0:1], TOP_EPS, None, ALU.add
                                        ).then_inc(consts, 1)
                dve.wait_ge(consts, 4)
                nc.vector.reciprocal(power_sum[:, 1:2], power_sum[:, 0:1]).then_inc(consts, 1)
                dve.wait_ge(consts, 5)
                ch.did(nc.vector.tensor_scalar(mix[:], power[:], power_sum[:, 1:2], escale[:],
                                               ALU.mult, ALU.mult))
                ch.end()

            dve.wait_ge(made, 4)
            nc.vector.tensor_copy(identb[:], ident32[:]).then_inc(consts, 1)
            nc.vector.tensor_copy(ident16[:], ident32[:]).then_inc(consts, 1)
            nc.vector.tensor_copy(iota[:], iota_i[:]).then_inc(consts, 1)
            max_ctx(0, 0)
            stats(0, 0)
            quant_ctx(0, 0, lambda: None)
            for j in range(1, NB):
                max_ctx(0, j)
                quant_ctx(0, j, lambda: dve.wait_ge(ctx_step, CTX_STEPS * j))
            quant_x(0, 0, lambda: dve.wait_ge(ctx_step, CTX_STEPS * NB))
            dve.wait_ge(consts, 3)
            mixes()
            max_w(0)
            max_w(1)
            scale_w(0)
            lo_w(0)
            attention(0, 0, 0)
            scale_w(1)
            norm2(0, 0)
            lo_w(1)
            max_w(2)
            scale_w(2)
            max_w(3)
            lo_w(2)
            top(0)
            combine(0, 0, -1)
            coefficients(0)
            for n in range(3, CHUNKS):
                scale_w(n)
                if n + 1 < CHUNKS:
                    max_w(n + 1)
                lo_w(n)

            def step(b, j, last):
                s, t = b * NB + j, b * NB + (j + 1)
                bt = b + 1 if j + 1 == NB else b
                front = not last or j + 1 < NB
                if not last:
                    max_ctx(b + 1, j)
                if front:
                    stats(t, j + 1)
                if not last:
                    quant_ctx(b + 1, j, lambda: dve.wait_ge(xq_step, XQ_STEPS * (s + 1)))
                combine(s, j, 0)
                if front:
                    quant_x(t, j + 1, (lambda: dve.wait_ge(xq_step, XQ_STEPS * t)) if last else
                            (lambda: dve.wait_ge(ctx_step, CTX_STEPS * (t + NB))))
                combine(s, j, 1, front)
                if front:
                    attention(t, j + 1, bt)
                combine(s, j, 2)
                if front:
                    norm2(t, j + 1)
                combine(s, j, 3)
                split_h(s, j)
                if front:
                    top(t)
                    combine(t, j + 1, -1)
                    coefficients(t)
                finish(s, j)

            by_batch(dve, step)


_INS = ["x", "ctx_2048", "L0_ffn_w_router", "L0_ffn_w_gate", "L0_ffn_w_up", "L0_ffn_w_down",
        "L0_ffn_amplitudes", "L0_ffn_expert_scale", "L0_ffn_shared_w_gate", "L0_ffn_shared_w_up",
        "L0_ffn_shared_w_down"]


def kernel(**inputs):
    import numpy as _np
    import concourse.bacc as _bacc
    from concourse import mybir as _mybir
    from concourse.bass_utils import run_bass_kernel_spmd as _run

    nc = _bacc.Bacc("TRN2", target_bir_lowering=False, num_devices=1)
    arrays, args = {}, []
    for name in _INS:
        a = _np.ascontiguousarray(inputs[name])
        arrays[f"in_{name}"] = a
        args.append(nc.dram_tensor(f"in_{name}", a.shape, _mybir.dt.from_np(a.dtype), kind="ExternalInput").ap())
    x = inputs["x"]
    args.append(nc.dram_tensor("out_0", x.shape, _mybir.dt.float32, kind="ExternalOutput").ap())
    build(nc, *args)
    r = _run(nc, [arrays], core_ids=[0])
    return r.results[0]["out_0"]
```

```python
from contextlib import ExitStack

import concourse.bass as bass
from concourse import mybir

ALU = mybir.AluOpType
ACT = mybir.ActivationFunctionType
AX = mybir.AxisListType
F32 = mybir.dt.float32
F16 = mybir.dt.float16
BF16 = mybir.dt.bfloat16
U32 = mybir.dt.uint32
I32 = mybir.dt.int32
ABSMAX = bass.bass_isa.ReduceOp.absmax

P = 128
EXPONENT = 0x7F800000
FP8_MAX = 448.0
FP8_TINY = 2.0 ** -6
ROUND = 1.5 * 2.0 ** 20
ACT_EPS = 1e-4
W_EPS = 1e-6
LN_EPS = 1e-5
TOP_EPS = 1e-8
LN_GAIN = 2.0 ** 10
TO_2_14 = 2.0 ** -14
SMALLEST = 1e-30


class Chain:

    def __init__(self, eng, sem, per_tile, t):
        self.eng, self.sem, self.per_tile, self.base, self.n = eng, sem, per_tile, per_tile * t, 0

    def did(self, instruction):
        instruction.then_inc(self.sem, 1)
        self.n += 1

    def sync(self, back=0):
        self.eng.wait_ge(self.sem, self.base + (self.n - back))

    def end(self):
        assert self.n == self.per_tile, (self.n, self.per_tile)


def settle(eng, passed):
    eng.sem_inc(passed, 1)


def wait_at(eng, sem, value):
    if not isinstance(value, int) or value > 0:
        eng.wait_ge(sem, value)


def build(nc, x, ctx, w_router, w_gate, w_up, w_down, amplitudes, expert_scale,
          s_gate, s_up, s_down, out):
    B, S, D = x.shape
    E = w_router.shape[1]
    I = w_down.shape[0]
    K = w_gate.shape[1] // I
    TOPK = 4
    KC = D // P
    NB = S // P
    TILES = B * NB
    CW = 512
    KPC = CW // I
    PAIRS = K // KPC
    IS = s_gate.shape[1]
    HW = I + IS
    HC = HW // P
    CHUNKS = 2 + 2 * (PAIRS + 1)
    DOWN = CHUNKS - 1
    assert IS == CW and D == CW and E == P and NB == 4
    STEPS = TILES // NB

    x_t = x.rearrange("b s d -> (b s) d")
    ctx_t = ctx.rearrange("b s d -> (b s) d")
    out_t = out.rearrange("b s d -> (b s) d")

    with ExitStack() as stack:
        def sb(name, shape, dt=F32):
            return stack.enter_context(nc.sbuf_tensor(name, shape, dt))

        def sem(name):
            return stack.enter_context(nc.semaphore(name))

        stage = [sb(f"stage{i}", [P, (HC if i == DOWN % 3 else KC) * CW]) for i in range(3)]
        wr = [sb(f"router_{h}", [P, KC, E], F16) for h in ("hi", "lo")]
        wgu = [sb(f"gate_up_{h}", [P, 2 * (PAIRS + 1), KC, CW], F16) for h in ("hi", "lo")]
        wd = [sb(f"down_{h}", [P, HC, D], F16) for h in ("hi", "lo")]
        w_max = sb("w_max", [P, CHUNKS])
        w_all = sb("w_all", [P, CHUNKS])
        w_tmp = sb("w_tmp", [P, CHUNKS])
        w_unscale = sb("w_unscale", [P, CHUNKS])
        w_scale = sb("w_scale", [P, CHUNKS])
        w_back = sb("w_back", [P, CHUNKS])
        ident32 = sb("ident32", [P, P])
        ident16 = sb("ident16", [P, P], F16)
        identb = sb("identb", [P, P], BF16)
        iota_i = sb("iota_i", [P, P], I32)
        iota = sb("iota", [P, P])
        minus_half = sb("minus_half", [P, 1])
        amp = sb("amp", [P, K, 2])
        amp_sq = sb("amp_sq", [P, K, 2])
        power = sb("power", [P, K])
        power_sum = sb("power_sum", [P, 2])
        escale = sb("escale", [P, 1])
        mix = sb("mix", [P, K])

        ctx_in = sb("ctx_in", [P, NB, D])
        ctx_max = sb("ctx_max", [P, 2, KC])
        ctx_all = sb("ctx_all", [P, 2, KC])
        ctx_safe = sb("ctx_safe", [P, 2, KC])
        ctx_rec = sb("ctx_rec", [P, 2, KC])
        ctx_mul = sb("ctx_mul", [P, 2, KC])
        ctx_m = sb("ctx_m", [P, 2, D])
        ctx_q = sb("ctx_q", [P, 2, D], BF16)
        ctx_qT = sb("ctx_qT", [P, B, KC, S], BF16)
        ctx_scale = sb("ctx_scale", [P, TILES, KC])

        x_in = sb("x_in", [P, 2, D])
        stat = sb("stat", [P, 6])
        mv = sb("mv", [P, 2])
        var = sb("var", [P, 1])
        neg_mean = sb("neg_mean", [P, 1])
        rstd = sb("rstd", [P, 1])
        y = sb("y", [P, D])
        x_max = sb("x_max", [P, KC])
        x_safe = sb("x_safe", [P, KC])
        x_rec = sb("x_rec", [P, KC])
        x_mul = sb("x_mul", [P, KC])
        x_scale = sb("x_scale", [P, KC])
        x_v = sb("x_v", [P, D])
        x_m = sb("x_m", [P, D])
        x_q = sb("x_q", [P, D], BF16)
        x_qT = sb("x_qT", [P, KC, P], BF16)
        both_scale = sb("both_scale", [P, NB, KC])
        x2 = sb("x2", [P, 2, D])
        stat2 = sb("stat2", [P, 6])
        mv2 = sb("mv2", [P, 2])
        var2 = sb("var2", [P, 1])
        neg_mean2 = sb("neg_mean2", [P, 1])
        gain2 = sb("gain2", [P, 1])
        shift2 = sb("shift2", [P, 1])
        y2 = sb("y2", [P, D])
        z = [sb(f"z_{h}", [P, D], F16) for h in ("hi", "lo")]
        zT = [sb(f"zT_{h}", [P, 2, KC, P], F16) for h in ("hi", "lo")]

        logit = sb("logit", [P, E])
        top8 = sb("top8", [P, 8])
        idx8 = sb("idx8", [P, 8], U32)
        idx = sb("idx", [P, TOPK])
        neg_max = sb("neg_max", [P, 1])
        prob = sb("prob", [P, E])
        prob_sum = sb("prob_sum", [P, 1])
        picked = [sb(f"picked{i}", [P, E]) for i in range(2)]
        weight = sb("weight", [P, E])
        weight_sum = sb("weight_sum", [P, 1])
        denom = sb("denom", [P, 1])
        inv_denom = sb("inv_denom", [P, 1])
        weightT = sb("weightT", [P, P])
        coef = sb("coef", [P, K])

        silu = sb("silu", [P, 2, CW])
        basis = sb("basis", [P, CW])
        hid = sb("hid", [P, 2, HW])
        hid_max = sb("hid_max", [P, 2])
        shared_top = sb("shared_top", [P, 1])
        hid_tmp = sb("hid_tmp", [P, 1])
        hid_unscale = sb("hid_unscale", [P, 1])
        hid_scale = sb("hid_scale", [P, 1])
        out_scale = sb("out_scale", [P, 1])
        hs = [sb(f"hs_{h}", [P, HW], F16) for h in ("hi", "lo")]
        hT = [sb(f"hT_{h}", [P, HC, P], F16) for h in ("hi", "lo")]
        y_out = sb("y_out", [P, 2, D])

        def bank(name):
            return stack.enter_context(nc.psum_tensor(name, [P, 512], F32))

        gate_ps = [bank("gate0"), bank("gate1")]
        up_ps = [bank("up0"), bank("up1")]
        turn_ps = [bank("turn0"), bank("turn1")]
        even_ps, odd_ps = bank("even"), bank("odd")
        turned = [t[:].bitcast(F16) for t in turn_ps]

        stage_in = [sem(f"stage_in{i}") for i in range(3)]
        small_in = sem("small_in")
        ctx_loaded = [sem(f"ctx_loaded{i}") for i in range(NB)]
        x_loaded = [sem(f"x_loaded{i}") for i in range(2)]
        made = sem("made")
        consts = sem("consts")
        passed_dve, passed_pool = sem("passed_dve"), sem("passed_pool")
        mix_step = sem("mix_step")
        w_maxed, w_reduced = sem("w_maxed"), sem("w_reduced")
        w_step, w_hi_done, w_ready = sem("w_step"), sem("w_hi_done"), sem("w_ready")
        ctx_maxed, ctx_reduced = sem("ctx_maxed"), sem("ctx_reduced")
        ctx_step, ctx_turned, ctx_kept = sem("ctx_step"), sem("ctx_turned"), sem("ctx_kept")
        ctx_scaled, ctx_mask, ctx_round = sem("ctx_scaled"), sem("ctx_mask"), sem("ctx_round")
        y_done, y2_done = sem("y_done"), sem("y2_done")
        shared_max = sem("shared_max")
        stat_step, rstd_done = sem("stat_step"), sem("rstd_done")
        xq_step, x_turned, x_kept = sem("xq_step"), sem("x_turned"), sem("x_kept")
        att_full, att_step = sem("att_full"), sem("att_step")
        ln_step, rstd2_done = sem("ln_step"), sem("rstd2_done")
        z_hi_done, z_turned, z_kept = sem("z_hi_done"), sem("z_turned"), sem("z_kept")
        logit_full, top_step, exp_done = sem("logit_full"), sem("top_step"), sem("exp_done")
        weight_turned, weightT_kept = sem("weight_turned"), sem("weightT_kept")
        coef_full, coef_done = sem("coef_full"), sem("coef_done")
        gate_full, up_full, silu_done = sem("gate_full"), sem("up_full"), sem("silu_done")
        pair_read, mix_acc = sem("pair_read"), sem("mix_acc")
        hid_step, h_hi_done = sem("hid_step"), sem("h_hi_done")
        h_turned, h_kept = sem("h_turned"), sem("h_kept")
        out_scaled = sem("out_scaled")
        down_full, down_read = sem("down_full"), sem("down_read")
        stored = [sem(f"stored{i}") for i in range(2)]

        CTX_STEPS, CTX_MASKS, CTX_ROUNDS = 4, 2, 2
        STAT_STEPS, RSTD_STEPS, XQ_STEPS, ATT_STEPS, LN_STEPS = 4, 2, 11, 16, 5
        TOP_STEPS, HID_STEPS, W_STEPS, MIX_STEPS, MIX_ACC = 12, 6, 4, 6, 8

        def use(t, p):
            return (PAIRS + 1) * t + (1 + p)

        def parity(j, p):
            return (j + 1 + p) % 2

        def chunk(p):
            return 1 + 2 * (p + 1)

        def ctx_in_step(j):
            return {1: (0, 1), 2: (2, 3)}.get(j, ())

        def by_round(eng, step):
            with eng.Fori(0, B - 1) as b:
                for j in range(1, NB + 1):
                    step(b, j, ctx_in_step(j), True, True)
            for j in range(1, NB):
                s = (B - 1) * NB + j
                step(B - 1, j, (), s + 1 < TILES, s + 2 < TILES)

        def w_part(h, n):
            if n == 0:
                return wr[h][:].rearrange("p c w -> p (c w)")
            if n == DOWN:
                return wd[h][:].rearrange("p c w -> p (c w)")
            return wgu[h][:, n - 1].rearrange("p c w -> p (c w)")

        def w_staged(n):
            width = KC * E if n == 0 else HC * D if n == DOWN else KC * CW
            return stage[n % 3][:, 0:width]

        block = stack.enter_context(nc.Block())

        @block.sync
        def _(sp):
            def load_ctx(b, k):
                if not isinstance(b, int) or b > 0:
                    sp.wait_ge(ctx_round, CTX_ROUNDS * (b * NB + k - NB) + CTX_ROUNDS)
                sp.dma_start(ctx_in[:, k, :], ctx_t[bass.ds((b * NB + k) * P, P), :]
                             ).then_inc(ctx_loaded[k], 16)

            def load_x(t, j):
                if not isinstance(t, int) or t >= 2:
                    sp.wait_ge(att_step, ATT_STEPS * (t - 2) + NB)
                sp.dma_start(x_in[:, j % 2, :], x_t[bass.ds(t * P, P), :]).then_inc(x_loaded[j % 2], 16)

            def load_chunk(n):
                if n >= 3:
                    sp.wait_ge(w_ready, n - 2)
                slot = stage[n % 3]

                def put(dst0, src):
                    kc = src.shape[0] // P
                    w = src.shape[1]
                    sp.dma_start(slot[:, dst0:dst0 + kc * w].rearrange("p (c w) -> p c w", c=kc),
                                 src.rearrange("(c p) w -> p c w", p=P)).then_inc(stage_in[n % 3], 16)

                if n == 0:
                    put(0, w_router)
                elif n == DOWN:
                    put(0, w_down)
                    put(I // P * D, s_down)
                else:
                    src = (s_gate, s_up) if n <= 2 else (w_gate, w_up)
                    col = 0 if n <= 2 else (n - 3) // 2 * CW
                    put(0, src[(n - 1) % 2][:, col:col + CW])

            load_ctx(0, 0)
            load_x(0, 0)
            for j in range(1, NB):
                load_ctx(0, j)
            load_chunk(0)
            sp.dma_start(amp[:], amplitudes).then_inc(small_in, 16)
            sp.dma_start(escale[:], expert_scale.rearrange("(e o) -> e o", o=1)).then_inc(small_in, 16)
            load_chunk(1)
            load_chunk(2)
            load_x(1, 1)
            for n in range(3, CHUNKS):
                load_chunk(n)
                if n == 4:
                    load_x(2, 2)

            def step(b, j, ctxs, front, ahead):
                for k in ctxs:
                    load_ctx(b + 1, k)
                if ahead:
                    load_x(b * NB + (j + 2), j)

            by_round(sp, step)

        @block.gpsimd
        def _(pool):
            nc.gpsimd.memset(minus_half[:], -0.5).then_inc(made, 1)
            nc.gpsimd.iota(iota_i[:], [[1, P]], base=0, channel_multiplier=0).then_inc(made, 1)
            nc.gpsimd.memset(ident32[:], 0.0).then_inc(made, 1)
            pool.wait_ge(made, 3)
            nc.gpsimd.affine_select(out=ident32[:], in_=ident32[:], compare_op=ALU.not_equal, fill=1.0,
                                    base=0, pattern=[[-1, P]], channel_multiplier=1).then_inc(made, 1)

            def reduce_ctx(c, k):
                pool.wait_ge(ctx_maxed, c + 1)
                settle(pool, passed_pool)
                nc.gpsimd.partition_all_reduce(ctx_all[:, k % 2], ctx_max[:, k % 2], P, ABSMAX
                                               ).then_inc(ctx_reduced, 1)

            def scale_ctx(c, k):
                pool.wait_ge(ctx_step, CTX_STEPS * (c + 1))
                c4 = lambda a: a.rearrange("p (c n) -> p c n", c=KC)
                nc.gpsimd.tensor_tensor(c4(ctx_in[:, k]), c4(ctx_in[:, k]),
                                        ctx_mul[:, k % 2].unsqueeze(2).to_broadcast([P, KC, P]), ALU.mult
                                        ).then_inc(ctx_scaled, 1)

            def round_ctx(c, k):
                ch = Chain(pool, ctx_round, CTX_ROUNDS, c)
                pool.wait_ge(ctx_mask, CTX_MASKS * (c + 1))
                ch.did(nc.gpsimd.tensor_tensor(ctx_in[:, k], ctx_in[:, k], ctx_m[:, k % 2], ALU.add))
                ch.sync()
                if not isinstance(c, int) or c >= 2:
                    pool.wait_ge(ctx_turned, c - 1)
                ch.did(nc.gpsimd.tensor_tensor(ctx_q[:, k % 2], ctx_in[:, k], ctx_m[:, k % 2], ALU.subtract))
                ch.end()

            def reduce_w(n):
                pool.wait_ge(w_maxed, n + 1)
                nc.gpsimd.partition_all_reduce(w_all[:, n:n + 1], w_max[:, n:n + 1], P, ABSMAX
                                               ).then_inc(w_reduced, 1)

            def rstd_of(t):
                pool.wait_ge(stat_step, STAT_STEPS * (t + 1))
                nc.gpsimd.tensor_tensor(rstd[:], var[:], minus_half[:], ALU.pow).then_inc(rstd_done, 1)

            def rstd2_of(t):
                ch = Chain(pool, rstd2_done, RSTD_STEPS, t)
                pool.wait_ge(ln_step, LN_STEPS * t + 4)
                ch.did(nc.gpsimd.tensor_tensor(gain2[:], var2[:], minus_half[:], ALU.pow))
                ch.sync()
                ch.did(nc.gpsimd.tensor_tensor(shift2[:], neg_mean2[:], gain2[:], ALU.mult))
                ch.end()

            for c in range(0, NB, 2):
                reduce_ctx(c, c)
                reduce_ctx(c + 1, c + 1)
                scale_ctx(c, c)
                scale_ctx(c + 1, c + 1)
                if c == 0:
                    rstd_of(0)
                round_ctx(c, c)
                round_ctx(c + 1, c + 1)
            reduce_w(0)
            reduce_w(1)
            rstd_of(1)
            rstd2_of(0)
            reduce_w(2)
            for n in range(3, 5):
                reduce_w(n)
            rstd_of(2)
            for n in range(5, 7):
                reduce_w(n)
            rstd2_of(1)
            for n in range(7, CHUNKS):
                reduce_w(n)

            def step(b, j, ctxs, front, ahead):
                s = b * NB + j
                for k in ctxs:
                    reduce_ctx((b + 1) * NB + k, k)
                if ahead:
                    rstd_of(s + 2)
                if front:
                    rstd2_of(s + 1)
                for k in ctxs:
                    scale_ctx((b + 1) * NB + k, k)
                for k in ctxs:
                    round_ctx((b + 1) * NB + k, k)

            by_round(pool, step)

        @block.scalar
        def _(act):
            def split_w(n):
                act.wait_ge(w_step, W_STEPS * (n + 1))
                dst = w_part(0, n)
                nc.scalar.activation(dst, w_staged(n), ACT.Copy, scale=w_scale[:, n:n + 1]
                                     ).then_inc(w_hi_done, 1)

            def keep_ctx(b, j):
                act.wait_ge(ctx_turned, b * NB + (j + 1))
                nc.scalar.copy(ctx_qT[:, b, :, j * P:(j + 1) * P] if isinstance(b, int) else
                               ctx_qT[:, bass.ds(b, 1), :, j * P:(j + 1) * P].rearrange("p o c n -> p (o c) n"),
                               turned[0].bitcast(BF16)[:, 0:KC * P].rearrange("p (c n) -> p c n", c=KC)
                               ).then_inc(ctx_kept, 1)

            def norm1(t, j):
                act.wait_ge(rstd_done, t + 1)
                wait_at(act, xq_step, XQ_STEPS * (t - 1) + 7 if not isinstance(t, int) or t else 0)
                nc.scalar.activation(y[:], x_in[:, j % 2, :], ACT.Identity, bias=neg_mean[:]).then_inc(y_done, 1)
                act.wait_ge(y_done, 2 * t + 1)
                nc.scalar.activation(y[:], y[:], ACT.Copy, scale=rstd[:]).then_inc(y_done, 1)

            def keep_x(t):
                act.wait_ge(x_turned, t + 1)
                wait_at(act, att_full, KC * t)
                nc.scalar.copy(x_qT[:].rearrange("p c n -> p (c n)"), turned[1].bitcast(BF16)[:, 0:KC * P]
                               ).then_inc(x_kept, 1)

            def norm2(t, j):
                act.wait_ge(rstd2_done, RSTD_STEPS * (t + 1))
                wait_at(act, ln_step, LN_STEPS * t)
                nc.scalar.activation(y2[:], x2[:, j % 2, :], ACT.Identity, bias=shift2[:], scale=gain2[:]
                                     ).then_inc(y2_done, 1)
                wait_at(act, z_turned, 2 * t)
                nc.scalar.activation(z[0][:], x2[:, j % 2, :], ACT.Identity, bias=shift2[:], scale=gain2[:]
                                     ).then_inc(z_hi_done, 1)

            def keep_z(t, j):
                for h in range(2):
                    act.wait_ge(z_turned, 2 * t + (h + 1))
                    nc.scalar.copy(zT[h][:, j % 2].rearrange("p c n -> p (c n)"), turned[h][:, 0:KC * P]
                                   ).then_inc(z_kept, 1)

            def exps(t):
                nc.scalar.preload_act_table(ACT.Exp)
                act.wait_ge(top_step, TOP_STEPS * t + 5)
                nc.scalar.activation(prob[:], logit[:], ACT.Exp, bias=neg_max[:], accum_out=prob_sum[:]
                                     ).then_inc(exp_done, 1)
                nc.scalar.preload_act_table(ACT.Silu)

            def keep_weight(t):
                act.wait_ge(weight_turned, t + 1)
                wait_at(act, coef_full, t)
                nc.scalar.copy(weightT[:], odd_ps[:, 0:P]).then_inc(weightT_kept, 1)

            def silus(t, j, p):
                k, par = use(t, p), parity(j, p)
                act.wait_ge(gate_full, k + 1)
                wait_at(act, pair_read, k)
                n = chunk(p)
                nc.scalar.activation(silu[:, par, :], gate_ps[par][:], ACT.Silu, scale=w_back[:, n:n + 1]
                                     ).then_inc(silu_done, 1)

            def h_hi(s, j):
                act.wait_ge(hid_step, HID_STEPS * s + 5)
                nc.scalar.activation(hs[0][:], hid[:, j % 2, :], ACT.Copy, scale=hid_scale[:]
                                     ).then_inc(h_hi_done, 1)

            def keep_h(s):
                for h in range(2):
                    act.wait_ge(h_turned, 2 * s + (h + 1))
                    nc.scalar.copy(hT[h][:].rearrange("p c n -> p (c n)"), turned[h][:, 0:HW]
                                   ).then_inc(h_kept, 1)

            def store(s, j):
                act.wait_ge(down_read, s + 2)
                act.dma_start(out_t[bass.ds(s * P, P), :], y_out[:, j % 2, :]).then_inc(stored[j % 2], 16)

            act.sem_inc(stored[0], 16)
            act.sem_inc(stored[1], 16)
            norm1(0, 0)
            for c in range(NB):
                keep_ctx(0, c)
            split_w(0)
            keep_x(0)
            split_w(1)
            norm2(0, 0)
            norm1(1, 1)
            keep_z(0, 0)
            split_w(2)
            exps(0)
            silus(0, 0, -1)
            keep_weight(0)

            def step(b, j, ctxs, front, ahead, weights=lambda p: None):
                s, t = b * NB + j, b * NB + (j + 1)
                if front:
                    keep_x(t)
                weights(0)
                silus(s, j, 0)
                if ahead:
                    norm1(s + 2, j)
                weights(1)
                silus(s, j, 1)
                if front:
                    norm2(t, j + 1)
                weights(2)
                silus(s, j, 2)
                if front:
                    keep_z(t, j + 1)
                for k in ctxs:
                    keep_ctx(b + 1, k)
                weights(3)
                silus(s, j, 3)
                if front:
                    exps(t)
                    keep_weight(t)
                h_hi(s, j)
                if front:
                    silus(t, j + 1, -1)
                weights(4)
                keep_h(s)
                store(s, j)

            step(0, 0, (), True, True, lambda p: [split_w(n) for n in range(3 + 2 * p, min(5 + 2 * p, CHUNKS))])
            by_round(act, step)
            act.wait_ge(stored[0], 16 * (TILES // 2) + 16)
            act.wait_ge(stored[1], 16 * (TILES // 2) + 16)

        @block.tensor
        def _(pe):
            HI_LO = ((0, 0), (0, 1), (1, 0))

            def turn_ctx(c, k):
                pe.wait_ge(ctx_round, CTX_ROUNDS * (c + 1))
                wait_at(pe, ctx_kept, c)
                ps = turned[0].bitcast(BF16)
                for kc in range(KC):
                    mm = nc.tensor.transpose(ps[:, kc * P:(kc + 1) * P], ctx_q[:, k % 2, kc * P:(kc + 1) * P], identb[:])
                mm.then_inc(ctx_turned, 1)

            def turn_x(t):
                pe.wait_ge(xq_step, XQ_STEPS * (t + 1))
                ps = turned[1].bitcast(BF16)
                for kc in range(KC):
                    mm = nc.tensor.transpose(ps[:, kc * P:(kc + 1) * P], x_q[:, kc * P:(kc + 1) * P], identb[:])
                mm.then_inc(x_turned, 1)

            def attend(t, b, kc):
                if kc == 0:
                    pe.wait_ge(x_kept, t + 1)
                    pe.wait_ge(ctx_kept, (b + 1) * NB)
                    wait_at(pe, down_read, t)
                elif kc == 1:
                    wait_at(pe, coef_done, t)
                else:
                    pe.wait_ge(att_step, ATT_STEPS * t + (kc - 1) * NB)
                ps = (even_ps, odd_ps)[kc % 2]
                rhs = (ctx_qT[:, b, kc, :] if isinstance(b, int) else
                       ctx_qT[:, bass.ds(b, 1), kc, :].rearrange("p o n -> p (o n)"))
                nc.tensor.matmul(ps[:], x_qT[:, kc, :], rhs, start=True, stop=True).then_inc(att_full, 1)

            def turn_z(t):
                for h in range(2):
                    if h == 0:
                        pe.wait_ge(z_hi_done, t + 1)
                    else:
                        pe.wait_ge(ln_step, LN_STEPS * (t + 1))
                    for kc in range(KC):
                        mm = nc.tensor.transpose(turned[h][:, kc * P:(kc + 1) * P],
                                                 z[h][:, kc * P:(kc + 1) * P], ident16[:])
                    mm.then_inc(z_turned, 1)

            def route(t, j):
                pe.wait_ge(z_kept, 2 * (t + 1))
                if isinstance(t, int) and t == 0:
                    pe.wait_ge(w_ready, 1)
                pe.wait_ge(att_step, ATT_STEPS * (t + 1))
                n = 0
                for kc in range(KC):
                    for a, w in HI_LO:
                        mm = nc.tensor.matmul(odd_ps[:, 0:E], zT[a][:, j % 2, kc, :], wr[w][:, kc, :],
                                              start=(n == 0), stop=(n == 3 * KC - 1))
                        n += 1
                mm.then_inc(logit_full, 1)

            def pair(t, j, p, between={}):
                k, par, n = use(t, p), parity(j, p), chunk(p)
                if 0 in between:
                    between[0]()
                wait_at(pe, pair_read, k)
                for i, (ps, full) in enumerate(((gate_ps[par], gate_full), (up_ps[par], up_full))):
                    if isinstance(t, int) and t == 0:
                        pe.wait_ge(w_ready, n + i + 1)
                    m = 0
                    for kc in range(KC):
                        if kc % 2 == 0 and i + kc > 0 and 2 * i + kc // 2 in between:
                            between[2 * i + kc // 2]()
                        for a, w in HI_LO:
                            mm = nc.tensor.matmul(ps[:], zT[a][:, j % 2, kc, :], wgu[w][:, n - 1 + i, kc, :],
                                                  start=(m == 0), stop=(m == 3 * KC - 1))
                            m += 1
                    mm.then_inc(full, 1)

            def turn_h(s, h):
                if h == 0:
                    pe.wait_ge(h_hi_done, s + 1)
                else:
                    pe.wait_ge(hid_step, HID_STEPS * (s + 1))
                for hc in range(HC):
                    mm = nc.tensor.transpose(turned[h][:, hc * P:(hc + 1) * P],
                                             hs[h][:, hc * P:(hc + 1) * P], ident16[:])
                mm.then_inc(h_turned, 1)

            def turn_weight(t):
                pe.wait_ge(top_step, TOP_STEPS * (t + 1) - 2)
                nc.tensor.transpose(odd_ps[:, 0:P], weight[:], ident32[:]).then_inc(weight_turned, 1)

            def coefs(t):
                pe.wait_ge(weightT_kept, t + 1)
                if isinstance(t, int) and t == 0:
                    pe.wait_ge(mix_step, MIX_STEPS)
                nc.tensor.matmul(odd_ps[:, 0:K], weightT[:], mix[:], start=True, stop=True
                                 ).then_inc(coef_full, 1)

            def down(s):
                if isinstance(s, int) and s == 0:
                    pe.wait_ge(w_ready, CHUNKS)
                n = 0
                for a, w in ((0, 0), (0, 1), (1, 0)):
                    if w == 0:
                        pe.wait_ge(h_kept, 2 * s + (a + 1))
                    for hc in range(HC):
                        mm = nc.tensor.matmul(even_ps[:], hT[a][:, hc, :], wd[w][:, hc, :],
                                              start=(n == 0), stop=(n == 3 * HC - 1))
                        n += 1
                mm.then_inc(down_full, 1)

            pe.wait_ge(consts, 3)
            for c in range(NB):
                turn_ctx(c, c)
            turn_x(0)
            for kc in range(KC):
                attend(0, 0, kc)
            turn_z(0)
            route(0, 0)
            pair(0, 0, -1)
            turn_weight(0)
            coefs(0)

            def step(b, j, ctxs, front, ahead):
                s, t = b * NB + j, b * NB + (j + 1)
                bt = b + 1 if j + 1 >= NB else b

                def attends(*kcs):
                    return lambda: [attend(t, bt, kc) for kc in kcs]

                def turn_ctxs():
                    pe.wait_ge(z_kept, 2 * (t + 1) - 1)
                    for k in ctxs:
                        turn_ctx((b + 1) * NB + k, k)

                if not front:
                    for p in range(PAIRS):
                        pair(s, j, p)
                    turn_h(s, 0)
                    turn_h(s, 1)
                    down(s)
                    return
                pair(s, j, 0, {0: lambda: turn_x(t), 2: attends(0, 1)})
                pair(s, j, 1, {0: attends(2, 3)})
                pair(s, j, 2, {3: lambda: turn_z(t)})
                pair(s, j, 3, {0: lambda: route(t, j + 1)} | ({1: turn_ctxs} if ctxs else {}))
                pair(t, j + 1, -1, {2: lambda: turn_weight(t), 3: lambda: turn_h(s, 0)})
                coefs(t)
                turn_h(s, 1)
                down(s)

            step(0, 0, (), True, True)
            by_round(pe, step)

        @block.vector
        def _(dve):
            dve.sem_inc(pair_read, 1)
            dve.sem_inc(down_read, 1)

            def max_ctx(b, k):
                dve.wait_ge(ctx_loaded[k], 16 * (b + 1))
                nc.vector.tensor_reduce(ctx_max[:, k % 2], ctx_in[:, k, :].rearrange("p (c n) -> p c n", c=KC),
                                        AX.X, ALU.max, apply_absolute_value=True).then_inc(ctx_maxed, 1)

            def scales_ctx(b, k):
                c = b * NB + k
                ch = Chain(dve, ctx_step, CTX_STEPS, c)
                dve.wait_ge(ctx_reduced, c + 1)
                ch.did(nc.vector.tensor_scalar(ctx_safe[:, k % 2], ctx_all[:, k % 2], W_EPS, None, ALU.max))
                ch.sync()
                ch.did(nc.vector.reciprocal(ctx_rec[:, k % 2], ctx_safe[:, k % 2]))
                ch.did(nc.vector.tensor_scalar(ctx_scale[:, bass.ds(c, 1), :].rearrange("p o c -> p (o c)"),
                                               ctx_safe[:, k % 2], 1.0 / FP8_MAX, None, ALU.mult))
                ch.sync(1)
                ch.did(nc.vector.tensor_scalar(ctx_mul[:, k % 2], ctx_rec[:, k % 2], FP8_MAX, None, ALU.mult))
                ch.end()

            def mask(ch, v, m):
                ch.did(nc.vector.tensor_scalar(m.bitcast(U32), v.bitcast(U32), EXPONENT, None,
                                               ALU.bitwise_and))
                ch.sync()
                ch.did(nc.vector.tensor_scalar(m, m, FP8_TINY, ROUND, ALU.max, ALU.mult))

            def mask_ctx(b, k):
                c = b * NB + k
                ch = Chain(dve, ctx_mask, CTX_MASKS, c)
                dve.wait_ge(ctx_scaled, c + 1)
                mask(ch, ctx_in[:, k], ctx_m[:, k % 2])
                ch.end()

            def stats(t, j):
                ch = Chain(dve, stat_step, STAT_STEPS, t)
                dve.wait_ge(x_loaded[j % 2], 16 * ((t - j % 2) // 2 + 1) if isinstance(t, int) else
                            (t - j % 2) * 8 + 16)
                ch.did(nc.vector.bn_stats(stat[:], x_in[:, j % 2, :]))
                ch.sync()
                settle(dve, passed_dve)
                ch.did(nc.vector.bn_aggr(mv[:], stat[:]))
                ch.sync()
                ch.did(nc.vector.tensor_scalar(var[:], mv[:, 1:2], LN_EPS, None, ALU.add))
                ch.did(nc.vector.tensor_scalar(neg_mean[:], mv[:, 0:1], -1.0, None, ALU.mult))
                ch.end()

            def quantise_x(t, b):
                ch = Chain(dve, xq_step, XQ_STEPS, t)
                c4 = lambda a: a.rearrange("p (c n) -> p c n", c=KC)
                dve.wait_ge(y_done, 2 * (t + 1))
                ch.did(nc.vector.tensor_reduce(x_max[:], c4(y[:]), AX.X, ALU.max, apply_absolute_value=True))
                ch.sync()
                ch.did(nc.vector.tensor_scalar(x_safe[:], x_max[:], ACT_EPS, None, ALU.max))
                ch.sync()
                ch.did(nc.vector.reciprocal(x_rec[:], x_safe[:]))
                ch.did(nc.vector.tensor_scalar(x_scale[:], x_safe[:], 1.0 / FP8_MAX, None, ALU.mult))
                ch.sync(1)
                ch.did(nc.vector.tensor_scalar(x_mul[:], x_rec[:], FP8_MAX, None, ALU.mult))
                ch.sync(1)
                dve.wait_ge(ctx_step, CTX_STEPS * (b + 1) * NB)
                ch.did(nc.vector.tensor_tensor(both_scale[:], ctx_scale[:, bass.ds(b * NB, NB), :],
                                               x_scale[:].unsqueeze(1).to_broadcast([P, NB, KC]), ALU.mult))
                ch.sync(1)
                ch.did(nc.vector.tensor_tensor(c4(x_v[:]), c4(y[:]), x_mul[:].unsqueeze(2).to_broadcast([P, KC, P]),
                                               ALU.mult))
                ch.sync()
                mask(ch, x_v[:], x_m[:])
                ch.sync()
                ch.did(nc.vector.tensor_tensor(x_v[:], x_v[:], x_m[:], ALU.add))
                ch.sync()
                wait_at(dve, x_turned, t)
                ch.did(nc.vector.tensor_tensor(x_q[:], x_v[:], x_m[:], ALU.subtract))
                ch.end()

            def attention(t, j):
                dve.wait_ge(xq_step, XQ_STEPS * t + 6)
                ch = Chain(dve, att_step, ATT_STEPS, t)
                for kc in range(KC):
                    dve.wait_ge(att_full, KC * t + (kc + 1))
                    ps = (even_ps, odd_ps)[kc % 2]
                    for nb in range(NB):
                        cols = slice(nb * P, (nb + 1) * P)
                        prev = x_in[:, j % 2, cols] if kc == 0 else x2[:, j % 2, cols]
                        if kc > 0:
                            ch.sync(NB - 1)
                        ch.did(nc.vector.scalar_tensor_tensor(x2[:, j % 2, cols], ps[:, cols],
                                                              both_scale[:, nb, kc:kc + 1], prev,
                                                              ALU.mult, ALU.add))
                ch.end()

            def stats2(t, j):
                ch = Chain(dve, ln_step, LN_STEPS, t)
                dve.wait_ge(att_step, ATT_STEPS * (t + 1))
                ch.did(nc.vector.bn_stats(stat2[:], x2[:, j % 2, :]))
                ch.sync()
                settle(dve, passed_dve)
                ch.did(nc.vector.bn_aggr(mv2[:], stat2[:]))
                ch.sync()
                ch.did(nc.vector.tensor_scalar(var2[:], mv2[:, 1:2], LN_EPS, LN_GAIN ** -2, ALU.add, ALU.mult))
                ch.did(nc.vector.tensor_scalar(neg_mean2[:], mv2[:, 0:1], -1.0, None, ALU.mult))
                return ch

            def z_lo(ch, t):
                dve.wait_ge(y2_done, t + 1)
                dve.wait_ge(z_hi_done, t + 1)
                wait_at(dve, z_turned, 2 * t)
                ch.did(nc.vector.tensor_tensor(z[1][:], y2[:], z[0][:], ALU.subtract))
                ch.end()

            def top(t):
                ch = Chain(dve, top_step, TOP_STEPS, t)
                dve.wait_ge(logit_full, t + 1)
                ch.did(nc.vector.tensor_scalar(logit[:], odd_ps[:, 0:E], w_back[:, 0:1], None, ALU.mult))
                ch.sync()
                settle(dve, passed_dve)
                ch.did(nc.vector.max(top8[:], logit[:]))
                ch.sync()
                settle(dve, passed_dve)
                ch.did(nc.vector.max_index(idx8[:], top8[:], logit[:]))
                ch.sync()
                ch.did(nc.vector.tensor_copy(idx[:], idx8[:, 0:TOPK]))
                ch.did(nc.vector.tensor_scalar(neg_max[:], top8[:, 0:1], -1.0, None, ALU.mult))
                ch.sync(1)
                ch.did(nc.vector.tensor_scalar(picked[0][:], iota[:], idx[:, 0:1], None, ALU.is_equal))
                for i in range(1, TOPK):
                    ch.sync()
                    ch.did(nc.vector.scalar_tensor_tensor(picked[i % 2][:], iota[:], idx[:, i:i + 1],
                                                          picked[(i - 1) % 2][:], ALU.is_equal, ALU.add))
                ch.sync()
                dve.wait_ge(exp_done, t + 1)
                ch.did(nc.vector.scalar_tensor_tensor(weight[:], picked[(TOPK - 1) % 2][:], 1.0, prob[:],
                                                      ALU.mult, ALU.mult, accum_out=weight_sum[:]))
                ch.sync()
                ch.did(nc.vector.scalar_tensor_tensor(denom[:], prob_sum[:], TOP_EPS, weight_sum[:],
                                                      ALU.mult, ALU.add))
                ch.sync()
                ch.did(nc.vector.reciprocal(inv_denom[:], denom[:]))
                ch.end()

            def coefficients(t):
                dve.wait_ge(coef_full, t + 1)
                dve.wait_ge(top_step, TOP_STEPS * (t + 1))
                nc.vector.tensor_scalar(coef[:], odd_ps[:, 0:K], inv_denom[:], None, ALU.mult
                                        ).then_inc(coef_done, 1)

            def combine(t, j, p):
                k, par, n = use(t, p), parity(j, p), chunk(p) + 1
                dve.wait_ge(up_full, k + 1)
                dve.wait_ge(silu_done, k + 1)
                dst = hid[:, j % 2, I:HW] if p < 0 else basis[:]
                if p > 0:
                    dve.wait_ge(mix_acc, MIX_ACC * t + KPC * p)
                nc.vector.scalar_tensor_tensor(dst, up_ps[par][:], w_back[:, n:n + 1], silu[:, par, :],
                                               ALU.mult, ALU.mult).then_inc(pair_read, 1)
                if p < 0:
                    dve.wait_ge(pair_read, k + 2)
                    nc.vector.tensor_reduce(shared_top[:, 0:1], hid[:, j % 2, I:HW], AX.X, ALU.max,
                                            apply_absolute_value=True).then_inc(shared_max, 1)
                    return
                dve.wait_ge(pair_read, k + 2)
                dve.wait_ge(coef_done, t + 1)
                mixed = hid[:, j % 2, 0:I]
                for i in range(KPC):
                    kk = p * KPC + i
                    part = basis[:, i * I:(i + 1) * I]
                    if kk == 0:
                        ins = nc.vector.tensor_scalar(mixed, part, coef[:, 0:1], None, ALU.mult)
                    else:
                        dve.wait_ge(mix_acc, MIX_ACC * t + kk)
                        ins = nc.vector.scalar_tensor_tensor(mixed, part, coef[:, kk:kk + 1], mixed,
                                                             ALU.mult, ALU.add)
                    ins.then_inc(mix_acc, 1)

            def split_h(s, j):
                ch = Chain(dve, hid_step, HID_STEPS, s)
                dve.wait_ge(mix_acc, MIX_ACC * (s + 1))
                dve.wait_ge(shared_max, s + 1)
                ch.did(nc.vector.tensor_scalar(hid_max[:, 0:1], shared_top[:], SMALLEST, None, ALU.max))
                ch.did(nc.vector.tensor_reduce(hid_max[:, 1:2], hid[:, j % 2, 0:I], AX.X, ALU.max,
                                               apply_absolute_value=True))
                ch.sync()
                ch.did(nc.vector.tensor_scalar(hid_tmp[:], hid_max[:, 1:2], hid_max[:, 0:1], TO_2_14,
                                               ALU.max, ALU.mult))
                ch.sync()
                ch.did(nc.vector.tensor_scalar(hid_unscale[:].bitcast(U32), hid_tmp[:].bitcast(U32),
                                               EXPONENT, None, ALU.bitwise_and))
                ch.sync()
                ch.did(nc.vector.reciprocal(hid_scale[:], hid_unscale[:]))
                dve.wait_ge(h_hi_done, s + 1)
                ch.did(nc.vector.scalar_tensor_tensor(hs[1][:], hid[:, j % 2, :], hid_scale[:], hs[0][:],
                                                      ALU.mult, ALU.subtract))
                ch.end()

            def finish(s, j):
                nc.vector.tensor_tensor(out_scale[:], hid_unscale[:], w_unscale[:, DOWN:DOWN + 1], ALU.mult
                                        ).then_inc(out_scaled, 1)
                dve.wait_ge(down_full, s + 1)
                dve.wait_ge(out_scaled, s + 1)
                dve.wait_ge(stored[j % 2], (s - j % 2) * 8 + 16)
                nc.vector.scalar_tensor_tensor(y_out[:, j % 2, :], even_ps[:], out_scale[:], x2[:, j % 2, :],
                                               ALU.mult, ALU.add).then_inc(down_read, 1)

            def max_w(n):
                dve.wait_ge(stage_in[n % 3], 16 * (n // 3 + 1) + (16 if n == DOWN else 0))
                nc.vector.tensor_reduce(w_max[:, n:n + 1], w_staged(n), AX.X, ALU.max,
                                        apply_absolute_value=True).then_inc(w_maxed, 1)

            def scale_w(n):
                ch = Chain(dve, w_step, W_STEPS, n)
                one = slice(n, n + 1)
                dve.wait_ge(w_reduced, n + 1)
                ch.did(nc.vector.tensor_scalar(w_tmp[:, one], w_all[:, one], SMALLEST, TO_2_14,
                                               ALU.max, ALU.mult))
                ch.sync()
                ch.did(nc.vector.tensor_scalar(w_unscale[:, one].bitcast(U32), w_tmp[:, one].bitcast(U32),
                                               EXPONENT, None, ALU.bitwise_and))
                ch.sync()
                ch.did(nc.vector.reciprocal(w_scale[:, one], w_unscale[:, one]))
                ch.did(nc.vector.tensor_scalar(w_back[:, one], w_unscale[:, one], 1.0 / LN_GAIN, None, ALU.mult))
                ch.end()

            def lo_w(n):
                dve.wait_ge(w_hi_done, n + 1)
                dve.wait_ge(w_step, W_STEPS * (n + 1))
                nc.vector.scalar_tensor_tensor(w_part(1, n), w_staged(n), w_scale[:, n:n + 1], w_part(0, n),
                                               ALU.mult, ALU.subtract).then_inc(w_ready, 1)

            def mixes():
                ch = Chain(dve, mix_step, MIX_STEPS, 0)
                dve.wait_ge(small_in, 32)
                ch.did(nc.vector.tensor_tensor(amp_sq[:], amp[:], amp[:], ALU.mult))
                ch.sync()
                ch.did(nc.vector.tensor_tensor(power[:], amp_sq[:, :, 0], amp_sq[:, :, 1], ALU.add))
                ch.sync()
                ch.did(nc.vector.tensor_reduce(power_sum[:, 0:1], power[:], AX.X, ALU.add))
                ch.sync()
                ch.did(nc.vector.tensor_scalar(power_sum[:, 0:1], power_sum[:, 0:1], TOP_EPS, None, ALU.add))
                ch.sync()
                ch.did(nc.vector.reciprocal(power_sum[:, 1:2], power_sum[:, 0:1]))
                ch.sync()
                ch.did(nc.vector.tensor_scalar(mix[:], power[:], power_sum[:, 1:2], escale[:],
                                               ALU.mult, ALU.mult))
                ch.end()

            dve.wait_ge(made, 4)
            nc.vector.tensor_copy(identb[:], ident32[:]).then_inc(consts, 1)
            nc.vector.tensor_copy(ident16[:], ident32[:]).then_inc(consts, 1)
            nc.vector.tensor_copy(iota[:], iota_i[:]).then_inc(consts, 1)
            max_ctx(0, 0)
            stats(0, 0)
            max_ctx(0, 1)
            scales_ctx(0, 0)
            scales_ctx(0, 1)
            mask_ctx(0, 0)
            max_ctx(0, 2)
            mask_ctx(0, 1)
            max_ctx(0, 3)
            scales_ctx(0, 2)
            scales_ctx(0, 3)
            quantise_x(0, 0)
            mask_ctx(0, 2)
            mixes()
            max_w(0)
            mask_ctx(0, 3)
            max_w(1)
            scale_w(0)
            scale_w(1)
            lo_w(0)
            stats(1, 1)
            attention(0, 0)
            ln = stats2(0, 0)
            lo_w(1)
            max_w(2)
            z_lo(ln, 0)
            scale_w(2)
            max_w(3)
            lo_w(2)
            quantise_x(1, 0)
            top(0)
            scale_w(3)
            max_w(4)
            combine(0, 0, -1)
            coefficients(0)

            def step(b, j, ctxs, front, ahead, weights=lambda p: None):
                s, t = b * NB + j, b * NB + (j + 1)
                bu = b + 1 if j + 2 >= NB else b
                for k in ctxs:
                    max_ctx(b + 1, k)
                if ahead:
                    stats(s + 2, j)
                weights(0)
                for k in ctxs:
                    scales_ctx(b + 1, k)
                if front:
                    attention(t, j + 1)
                combine(s, j, 0)
                if front:
                    ln = stats2(t, j + 1)
                weights(1)
                combine(s, j, 1)
                if front:
                    z_lo(ln, t)
                if ahead:
                    quantise_x(s + 2, bu)
                weights(2)
                combine(s, j, 2)
                for k in ctxs:
                    mask_ctx(b + 1, k)
                weights(3)
                if front:
                    top(t)
                combine(s, j, 3)
                split_h(s, j)
                weights(4)
                if front:
                    coefficients(t)
                    combine(t, j + 1, -1)
                finish(s, j)

            def split_weights(p):
                for n in range(3 + 2 * p, min(5 + 2 * p, CHUNKS)):
                    if n > 3:
                        scale_w(n)
                    if 4 < n + 1 < CHUNKS:
                        max_w(n + 1)
                    lo_w(n)

            step(0, 0, (), True, True, split_weights)
            by_round(dve, step)


_INS = ["x", "ctx_2048", "L0_ffn_w_router", "L0_ffn_w_gate", "L0_ffn_w_up", "L0_ffn_w_down",
        "L0_ffn_amplitudes", "L0_ffn_expert_scale", "L0_ffn_shared_w_gate", "L0_ffn_shared_w_up",
        "L0_ffn_shared_w_down"]


def kernel(**inputs):
    import numpy as _np
    import concourse.bacc as _bacc
    from concourse import mybir as _mybir
    from concourse.bass_utils import run_bass_kernel_spmd as _run

    nc = _bacc.Bacc("TRN2", target_bir_lowering=False, num_devices=1)
    arrays, args = {}, []
    for name in _INS:
        a = _np.ascontiguousarray(inputs[name])
        arrays[f"in_{name}"] = a
        args.append(nc.dram_tensor(f"in_{name}", a.shape, _mybir.dt.from_np(a.dtype), kind="ExternalInput").ap())
    x = inputs["x"]
    args.append(nc.dram_tensor("out_0", x.shape, _mybir.dt.float32, kind="ExternalOutput").ap())
    build(nc, *args)
    r = _run(nc, [arrays], core_ids=[0])
    return r.results[0]["out_0"]
```

```python
from contextlib import ExitStack

import concourse.bass as bass
from concourse import mybir

ALU = mybir.AluOpType
ACT = mybir.ActivationFunctionType
AX = mybir.AxisListType
F32 = mybir.dt.float32
F16 = mybir.dt.float16
BF16 = mybir.dt.bfloat16
U32 = mybir.dt.uint32
I32 = mybir.dt.int32
ABSMAX = bass.bass_isa.ReduceOp.absmax

P = 128
EXPONENT = 0x7F800000
FP8_MAX = 448.0
FP8_TINY = 2.0 ** -6
ROUND = 1.5 * 2.0 ** 20
ACT_EPS = 1e-4
W_EPS = 1e-6
LN_EPS = 1e-5
TOP_EPS = 1e-8
LN_GAIN = 2.0 ** 10
TO_2_14 = 2.0 ** -14
SMALLEST = 1e-30


class Chain:

    def __init__(self, eng, sem, per_tile, t):
        self.eng, self.sem, self.per_tile, self.base, self.n = eng, sem, per_tile, per_tile * t, 0

    def did(self, instruction):
        instruction.then_inc(self.sem, 1)
        self.n += 1

    def sync(self, back=0):
        self.eng.wait_ge(self.sem, self.base + (self.n - back))

    def end(self):
        assert self.n == self.per_tile, (self.n, self.per_tile)


def settle(eng, passed):
    eng.sem_inc(passed, 1)


def wait_at(eng, sem, value):
    if not isinstance(value, int) or value > 0:
        eng.wait_ge(sem, value)


def build(nc, x, ctx, w_router, w_gate, w_up, w_down, amplitudes, expert_scale,
          s_gate, s_up, s_down, out):
    B, S, D = x.shape
    E = w_router.shape[1]
    I = w_down.shape[0]
    K = w_gate.shape[1] // I
    TOPK = 4
    KC = D // P
    NB = S // P
    TILES = B * NB
    CW = 512
    KPC = CW // I
    PAIRS = K // KPC
    IS = s_gate.shape[1]
    HW = I + IS
    HC = HW // P
    CHUNKS = 2 + 2 * (PAIRS + 1)
    DOWN = CHUNKS - 1
    MAX_BY_DVE = ()
    assert IS == CW and D == CW and E == P and NB == 4
    STEPS = TILES // NB

    def slot_of(n):
        return (n - 1) % 3

    x_t = x.rearrange("b s d -> (b s) d")
    ctx_t = ctx.rearrange("b s d -> (b s) d")
    out_t = out.rearrange("b s d -> (b s) d")

    with ExitStack() as stack:
        def sb(name, shape, dt=F32):
            return stack.enter_context(nc.sbuf_tensor(name, shape, dt))

        def sem(name):
            return stack.enter_context(nc.semaphore(name))

        stage = [sb(f"stage{i}", [P, (HC if i == slot_of(DOWN) else KC) * CW]) for i in range(3)]
        wr = [sb(f"router_{h}", [P, KC, E], F16) for h in ("hi", "lo")]
        wgu = [sb(f"gate_up_{h}", [P, 2 * (PAIRS + 1), KC, CW], F16) for h in ("hi", "lo")]
        wd = [sb(f"down_{h}", [P, HC, D], F16) for h in ("hi", "lo")]
        w_max = sb("w_max", [P, CHUNKS])
        w_all = sb("w_all", [P, CHUNKS])
        w_tmp = sb("w_tmp", [P, CHUNKS])
        w_unscale = sb("w_unscale", [P, CHUNKS])
        w_scale = sb("w_scale", [P, CHUNKS])
        w_back = sb("w_back", [P, CHUNKS])
        ident32 = sb("ident32", [P, P])
        ident16 = sb("ident16", [P, P], F16)
        identb = sb("identb", [P, P], BF16)
        iota_i = sb("iota_i", [P, P], I32)
        iota = sb("iota", [P, P])
        minus_half = sb("minus_half", [P, 1])
        amp = sb("amp", [P, K, 2])
        amp_sq = sb("amp_sq", [P, K, 2])
        power = sb("power", [P, K])
        power_sum = sb("power_sum", [P, 2])
        escale = sb("escale", [P, 1])
        mix = sb("mix", [P, K])

        ctx_in = sb("ctx_in", [P, NB, D])
        ctx_max = sb("ctx_max", [P, NB, KC])
        ctx_all = sb("ctx_all", [P, NB, KC])
        ctx_safe = sb("ctx_safe", [P, NB, KC])
        ctx_rec = sb("ctx_rec", [P, NB, KC])
        ctx_mul = sb("ctx_mul", [P, NB, KC])
        ctx_m = sb("ctx_m", [P, 2, D])
        ctx_q = sb("ctx_q", [P, 2, D], BF16)
        ctx_qT = sb("ctx_qT", [P, B, KC, S], BF16)
        ctx_scale = sb("ctx_scale", [P, TILES, KC])

        x_in = sb("x_in", [P, 2, D])
        stat = sb("stat", [P, 6])
        mv = sb("mv", [P, 2])
        var = sb("var", [P, 1])
        neg_mean = sb("neg_mean", [P, 1])
        rstd = sb("rstd", [P, 1])
        y = sb("y", [P, D])
        x_max = sb("x_max", [P, KC])
        x_safe = sb("x_safe", [P, KC])
        x_rec = sb("x_rec", [P, KC])
        x_mul = sb("x_mul", [P, KC])
        x_scale = sb("x_scale", [P, KC])
        x_v = sb("x_v", [P, D])
        x_m = sb("x_m", [P, D])
        x_q = sb("x_q", [P, D], BF16)
        x_qT = sb("x_qT", [P, KC, P], BF16)
        both_scale = sb("both_scale", [P, NB, KC])
        x2 = sb("x2", [P, 2, D])
        stat2 = sb("stat2", [P, 6])
        mv2 = sb("mv2", [P, 2])
        var2 = sb("var2", [P, 1])
        neg_mean2 = sb("neg_mean2", [P, 1])
        gain2 = sb("gain2", [P, 1])
        shift2 = sb("shift2", [P, 1])
        y2 = sb("y2", [P, D])
        z = [sb(f"z_{h}", [P, D], F16) for h in ("hi", "lo")]
        zT = [sb(f"zT_{h}", [P, 2, KC, P], F16) for h in ("hi", "lo")]

        logit = sb("logit", [P, E])
        top8 = sb("top8", [P, 8])
        idx8 = sb("idx8", [P, 8], U32)
        idx = sb("idx", [P, TOPK])
        neg_max = sb("neg_max", [P, 1])
        prob = sb("prob", [P, E])
        prob_sum = sb("prob_sum", [P, 1])
        picked = [sb(f"picked{i}", [P, E]) for i in range(2)]
        weight = sb("weight", [P, E])
        weight_sum = sb("weight_sum", [P, 1])
        denom = sb("denom", [P, 1])
        inv_denom = sb("inv_denom", [P, 1])
        weightT = sb("weightT", [P, P])
        coef = sb("coef", [P, K])

        silu = sb("silu", [P, 2, CW])
        basis = sb("basis", [P, CW])
        hid = sb("hid", [P, 2, HW])
        hid_max = sb("hid_max", [P, 2])
        shared_top = sb("shared_top", [P, 1])
        hid_tmp = sb("hid_tmp", [P, 1])
        hid_unscale = sb("hid_unscale", [P, 1])
        hid_scale = sb("hid_scale", [P, 1])
        out_scale = sb("out_scale", [P, 1])
        hs = [sb(f"hs_{h}", [P, HW], F16) for h in ("hi", "lo")]
        hT = [sb(f"hT_{h}", [P, HC, P], F16) for h in ("hi", "lo")]
        y_out = sb("y_out", [P, 2, D])

        def bank(name):
            return stack.enter_context(nc.psum_tensor(name, [P, 512], F32))

        gate_ps = [bank("gate0"), bank("gate1")]
        up_ps = [bank("up0"), bank("up1")]
        turn_ps = [bank("turn0"), bank("turn1")]
        even_ps, odd_ps = bank("even"), bank("odd")
        turned = [t[:].bitcast(F16) for t in turn_ps]

        stage_in = [sem(f"stage_in{i}") for i in range(3)]
        router_in, small_in = sem("router_in"), sem("small_in")
        ctx_loaded = [sem(f"ctx_loaded{i}") for i in range(NB)]
        x_loaded = [sem(f"x_loaded{i}") for i in range(2)]
        made = sem("made")
        consts = sem("consts")
        passed_dve, passed_pool = sem("passed_dve"), sem("passed_pool")
        mix_step = sem("mix_step")
        w_maxed, w_summed, w_reduced = sem("w_maxed"), sem("w_summed"), sem("w_reduced")
        w_step, w_hi_done, w_ready = sem("w_step"), sem("w_hi_done"), sem("w_ready")
        ctx_maxed, ctx_reduced = sem("ctx_maxed"), sem("ctx_reduced")
        ctx_step, ctx_turned, ctx_kept = sem("ctx_step"), sem("ctx_turned"), sem("ctx_kept")
        ctx_scaled, ctx_mask, ctx_round = sem("ctx_scaled"), sem("ctx_mask"), sem("ctx_round")
        y_done, y2_done = sem("y_done"), sem("y2_done")
        shared_max = sem("shared_max")
        stat_step, rstd_done = sem("stat_step"), sem("rstd_done")
        xq_step, x_turned, x_kept = sem("xq_step"), sem("x_turned"), sem("x_kept")
        att_full, att_step = sem("att_full"), sem("att_step")
        ln_step, rstd2_done = sem("ln_step"), sem("rstd2_done")
        z_hi_done, z_turned, z_kept = sem("z_hi_done"), sem("z_turned"), sem("z_kept")
        logit_full, top_step, exp_done = sem("logit_full"), sem("top_step"), sem("exp_done")
        weight_turned, weightT_kept = sem("weight_turned"), sem("weightT_kept")
        coef_full, coef_done = sem("coef_full"), sem("coef_done")
        gate_full, up_full, silu_done = sem("gate_full"), sem("up_full"), sem("silu_done")
        pair_read, mix_acc = sem("pair_read"), sem("mix_acc")
        hid_step, h_hi_done = sem("hid_step"), sem("h_hi_done")
        h_turned, h_kept = sem("h_turned"), sem("h_kept")
        out_scaled = sem("out_scaled")
        down_full, down_read = sem("down_full"), sem("down_read")
        stored = [sem(f"stored{i}") for i in range(2)]

        CTX_STEPS, CTX_MASKS, CTX_ROUNDS = 4, 2, 2
        STAT_STEPS, RSTD_STEPS, XQ_STEPS, ATT_STEPS, LN_STEPS = 4, 2, 11, 16, 5
        TOP_STEPS, HID_STEPS, W_STEPS, MIX_STEPS, MIX_ACC = 12, 6, 4, 6, 8

        def use(t, p):
            return (PAIRS + 1) * t + (1 + p)

        def parity(j, p):
            return (j + 1 + p) % 2

        def chunk(p):
            return 1 + 2 * (p + 1)

        def ctx_in_step(j):
            return {1: (0, 1), 2: (2, 3)}.get(j, ())

        def turned_ctxs(b, j):
            return () if isinstance(b, int) else ctx_in_step(j - 1)

        def by_round(eng, step):
            with eng.Fori(0, B - 1) as b:
                for j in range(1, NB + 1):
                    step(b, j, ctx_in_step(j), True, True)
            for j in range(1, NB):
                s = (B - 1) * NB + j
                step(B - 1, j, (), s + 1 < TILES, s + 2 < TILES)

        def w_part(h, n):
            if n == 0:
                return wr[h][:].rearrange("p c w -> p (c w)")
            if n == DOWN:
                return wd[h][:].rearrange("p c w -> p (c w)")
            return wgu[h][:, n - 1].rearrange("p c w -> p (c w)")

        def w_staged(n):
            width = KC * E if n == 0 else HC * D if n == DOWN else KC * CW
            return y_out[:, 1, :] if n == 0 else stage[slot_of(n)][:, 0:width]

        def wait_staged(eng, n):
            if n == 0:
                eng.wait_ge(router_in, 16)
            else:
                eng.wait_ge(stage_in[slot_of(n)], 16 * ((n - 1) // 3 + 1) + (16 if n == DOWN else 0))

        block = stack.enter_context(nc.Block())

        @block.sync
        def _(sp):
            def load_ctx(b, k):
                if not isinstance(b, int) or b > 0:
                    sp.wait_ge(ctx_round, CTX_ROUNDS * (b * NB + k - NB) + CTX_ROUNDS)
                sp.dma_start(ctx_in[:, k, :], ctx_t[bass.ds((b * NB + k) * P, P), :]
                             ).then_inc(ctx_loaded[k], 16)

            def load_x(t, j):
                if not isinstance(t, int) or t >= 2:
                    sp.wait_ge(att_step, ATT_STEPS * (t - 2) + NB)
                sp.dma_start(x_in[:, j % 2, :], x_t[bass.ds(t * P, P), :]).then_inc(x_loaded[j % 2], 16)

            def load_chunk(n):
                if n == 0:
                    sp.dma_start(y_out[:, 1, :].rearrange("p (c w) -> p c w", c=KC),
                                 w_router.rearrange("(c p) w -> p c w", p=P)).then_inc(router_in, 16)
                    return
                if n >= 4:
                    sp.wait_ge(w_ready, n - 2)
                slot = stage[slot_of(n)]

                def put(dst0, src):
                    kc = src.shape[0] // P
                    w = src.shape[1]
                    sp.dma_start(slot[:, dst0:dst0 + kc * w].rearrange("p (c w) -> p c w", c=kc),
                                 src.rearrange("(c p) w -> p c w", p=P)).then_inc(stage_in[slot_of(n)], 16)

                if n == DOWN:
                    put(0, w_down)
                    put(I // P * D, s_down)
                else:
                    src = (s_gate, s_up) if n <= 2 else (w_gate, w_up)
                    col = 0 if n <= 2 else (n - 3) // 2 * CW
                    put(0, src[(n - 1) % 2][:, col:col + CW])

            def store(s, j):
                sp.wait_ge(down_read, s + 2)
                sp.dma_start(out_t[bass.ds(s * P, P), :], y_out[:, j % 2, :]).then_inc(stored[j % 2], 16)

            sp.sem_inc(stored[0], 16)
            sp.sem_inc(stored[1], 16)
            load_ctx(0, 0)
            load_x(0, 0)
            for j in range(1, NB):
                load_ctx(0, j)
            load_chunk(0)
            sp.dma_start(amp[:], amplitudes).then_inc(small_in, 16)
            sp.dma_start(escale[:], expert_scale.rearrange("(e o) -> e o", o=1)).then_inc(small_in, 16)
            load_chunk(1)
            load_chunk(2)
            load_chunk(3)
            load_x(1, 1)
            for n in range(4, CHUNKS):
                load_chunk(n)
                if n == 4:
                    load_x(2, 2)

            def step(b, j, ctxs, front, ahead):
                for k in ctxs:
                    load_ctx(b + 1, k)
                if ahead:
                    load_x(b * NB + (j + 2), j)
                store(b * NB + (j - 1), j - 1)

            by_round(sp, step)
            store(TILES - 1, TILES - 1)
            sp.wait_ge(stored[0], 16 * (TILES // 2) + 16)
            sp.wait_ge(stored[1], 16 * (TILES // 2) + 16)

        @block.gpsimd
        def _(pool):
            nc.gpsimd.memset(minus_half[:], -0.5).then_inc(made, 1)
            nc.gpsimd.iota(iota_i[:], [[1, P]], base=0, channel_multiplier=0).then_inc(made, 1)
            nc.gpsimd.memset(ident32[:], 0.0).then_inc(made, 1)
            pool.wait_ge(made, 3)
            nc.gpsimd.affine_select(out=ident32[:], in_=ident32[:], compare_op=ALU.not_equal, fill=1.0,
                                    base=0, pattern=[[-1, P]], channel_multiplier=1).then_inc(made, 1)

            def reduce_ctx(c, k):
                pool.wait_ge(ctx_maxed, c + 1)
                settle(pool, passed_pool)
                nc.gpsimd.partition_all_reduce(ctx_all[:, k], ctx_max[:, k], P, ABSMAX
                                               ).then_inc(ctx_reduced, 1)

            def scale_ctx(c, k):
                pool.wait_ge(ctx_step, CTX_STEPS * (c + 1))
                c4 = lambda a: a.rearrange("p (c n) -> p c n", c=KC)
                nc.gpsimd.tensor_tensor(c4(ctx_in[:, k]), c4(ctx_in[:, k]),
                                        ctx_mul[:, k].unsqueeze(2).to_broadcast([P, KC, P]), ALU.mult
                                        ).then_inc(ctx_scaled, 1)

            def round_ctx(c, k):
                ch = Chain(pool, ctx_round, CTX_ROUNDS, c)
                pool.wait_ge(ctx_mask, CTX_MASKS * (c + 1))
                ch.did(nc.gpsimd.tensor_tensor(ctx_in[:, k], ctx_in[:, k], ctx_m[:, k % 2], ALU.add))
                ch.sync()
                if not isinstance(c, int) or c >= 2:
                    pool.wait_ge(ctx_turned, c - 1)
                ch.did(nc.gpsimd.tensor_tensor(ctx_q[:, k % 2], ctx_in[:, k], ctx_m[:, k % 2], ALU.subtract))
                ch.end()

            def reduce_w(n):
                if n in MAX_BY_DVE:
                    pool.wait_ge(w_maxed, MAX_BY_DVE.index(n) + 1)
                else:
                    pool.wait_ge(w_summed, n + 1 - len([m for m in MAX_BY_DVE if m < n]))
                nc.gpsimd.partition_all_reduce(w_all[:, n:n + 1], w_max[:, n:n + 1], P, ABSMAX
                                               ).then_inc(w_reduced, 1)

            def rstd_of(t):
                pool.wait_ge(stat_step, STAT_STEPS * (t + 1))
                nc.gpsimd.tensor_tensor(rstd[:], var[:], minus_half[:], ALU.pow).then_inc(rstd_done, 1)

            def rstd2_of(t):
                ch = Chain(pool, rstd2_done, RSTD_STEPS, t)
                pool.wait_ge(ln_step, LN_STEPS * t + 4)
                ch.did(nc.gpsimd.tensor_tensor(gain2[:], var2[:], minus_half[:], ALU.pow))
                ch.sync()
                ch.did(nc.gpsimd.tensor_tensor(shift2[:], neg_mean2[:], gain2[:], ALU.mult))
                ch.end()

            reduce_ctx(0, 0)
            rstd_of(0)
            reduce_ctx(1, 1)
            round_ctx(0, 0)
            reduce_w(0)
            reduce_ctx(2, 2)
            reduce_ctx(3, 3)
            round_ctx(1, 1)
            round_ctx(2, 2)
            reduce_w(1)
            round_ctx(3, 3)
            for n in range(2, 4):
                reduce_w(n)
            rstd2_of(0)
            rstd_of(1)
            reduce_w(4)
            rstd_of(2)
            reduce_w(5)
            reduce_w(6)
            rstd2_of(1)
            for n in range(7, CHUNKS):
                reduce_w(n)

            def step(b, j, ctxs, front, ahead):
                s = b * NB + j
                for k in ctxs:
                    reduce_ctx((b + 1) * NB + k, k)
                if ahead:
                    rstd_of(s + 2)
                if front:
                    rstd2_of(s + 1)
                for k in ctxs:
                    scale_ctx((b + 1) * NB + k, k)
                for k in ctxs:
                    round_ctx((b + 1) * NB + k, k)

            by_round(pool, step)

        @block.scalar
        def _(act):
            def sum_w(n):
                if n in MAX_BY_DVE:
                    return
                wait_staged(act, n)
                nc.scalar.activation(w_part(0, n).bitcast(BF16), w_staged(n), ACT.Abs,
                                     accum_out=w_max[:, n:n + 1]).then_inc(w_summed, 1)

            def scale_ctx(c, k):
                act.wait_ge(ctx_step, CTX_STEPS * (c + 1))
                for kc in range(KC):
                    part = ctx_in[:, k, kc * P:(kc + 1) * P]
                    ins = nc.scalar.activation(part, part, ACT.Copy, scale=ctx_mul[:, k, kc:kc + 1])
                ins.then_inc(ctx_scaled, 1)

            def split_w(n):
                act.wait_ge(w_step, W_STEPS * (n + 1))
                dst = w_part(0, n)
                nc.scalar.activation(dst, w_staged(n), ACT.Copy, scale=w_scale[:, n:n + 1]
                                     ).then_inc(w_hi_done, 1)

            def keep_ctx(b, j):
                act.wait_ge(ctx_turned, b * NB + (j + 1))
                nc.scalar.copy(ctx_qT[:, b, :, j * P:(j + 1) * P] if isinstance(b, int) else
                               ctx_qT[:, bass.ds(b, 1), :, j * P:(j + 1) * P].rearrange("p o c n -> p (o c) n"),
                               turned[0].bitcast(BF16)[:, 0:KC * P].rearrange("p (c n) -> p c n", c=KC)
                               ).then_inc(ctx_kept, 1)

            def norm1(t, j):
                act.wait_ge(rstd_done, t + 1)
                wait_at(act, xq_step, XQ_STEPS * (t - 1) + 7 if not isinstance(t, int) or t else 0)
                nc.scalar.activation(y[:], x_in[:, j % 2, :], ACT.Identity, bias=neg_mean[:]).then_inc(y_done, 1)
                act.wait_ge(y_done, 2 * t + 1)
                nc.scalar.activation(y[:], y[:], ACT.Copy, scale=rstd[:]).then_inc(y_done, 1)

            def keep_x(t):
                act.wait_ge(x_turned, t + 1)
                wait_at(act, att_full, KC * t)
                nc.scalar.copy(x_qT[:].rearrange("p c n -> p (c n)"), turned[1].bitcast(BF16)[:, 0:KC * P]
                               ).then_inc(x_kept, 1)

            def norm2(t, j):
                act.wait_ge(rstd2_done, RSTD_STEPS * (t + 1))
                wait_at(act, ln_step, LN_STEPS * t)
                nc.scalar.activation(y2[:], x2[:, j % 2, :], ACT.Identity, bias=shift2[:], scale=gain2[:]
                                     ).then_inc(y2_done, 1)
                wait_at(act, z_turned, 2 * t)
                nc.scalar.activation(z[0][:], x2[:, j % 2, :], ACT.Identity, bias=shift2[:], scale=gain2[:]
                                     ).then_inc(z_hi_done, 1)

            def keep_z(t, j):
                for h in range(2):
                    act.wait_ge(z_turned, 2 * t + (h + 1))
                    nc.scalar.copy(zT[h][:, j % 2].rearrange("p c n -> p (c n)"), turned[h][:, 0:KC * P]
                                   ).then_inc(z_kept, 1)

            def exps(t):
                nc.scalar.preload_act_table(ACT.Exp)
                act.wait_ge(top_step, TOP_STEPS * t + 5)
                nc.scalar.activation(prob[:], logit[:], ACT.Exp, bias=neg_max[:], accum_out=prob_sum[:]
                                     ).then_inc(exp_done, 1)
                nc.scalar.preload_act_table(ACT.Silu)

            def keep_weight(t):
                act.wait_ge(weight_turned, t + 1)
                wait_at(act, coef_full, t)
                nc.scalar.copy(weightT[:], odd_ps[:, 0:P]).then_inc(weightT_kept, 1)

            def silus(t, j, p):
                k, par = use(t, p), parity(j, p)
                act.wait_ge(gate_full, k + 1)
                wait_at(act, pair_read, k)
                n = chunk(p)
                nc.scalar.activation(silu[:, par, :], gate_ps[par][:], ACT.Silu, scale=w_back[:, n:n + 1]
                                     ).then_inc(silu_done, 1)

            def h_hi(s, j):
                act.wait_ge(hid_step, HID_STEPS * s + 5)
                nc.scalar.activation(hs[0][:], hid[:, j % 2, :], ACT.Copy, scale=hid_scale[:]
                                     ).then_inc(h_hi_done, 1)

            def keep_h(s):
                for h in range(2):
                    act.wait_ge(h_turned, 2 * s + (h + 1))
                    nc.scalar.copy(hT[h][:].rearrange("p c n -> p (c n)"), turned[h][:, 0:HW]
                                   ).then_inc(h_kept, 1)

            norm1(0, 0)
            sum_w(0)
            scale_ctx(2, 2)
            scale_ctx(3, 3)
            sum_w(1)
            keep_ctx(0, 0)
            split_w(0)
            keep_ctx(0, 1)
            sum_w(2)
            keep_ctx(0, 2)
            split_w(1)
            keep_x(0)
            keep_ctx(0, 3)
            sum_w(3)
            split_w(2)
            norm2(0, 0)
            norm1(1, 1)
            keep_z(0, 0)
            sum_w(4)
            split_w(3)
            exps(0)
            silus(0, 0, -1)

            def step(b, j, ctxs, front, ahead, weights=lambda p: None):
                s, t = b * NB + j, b * NB + (j + 1)
                if front:
                    keep_x(t)
                keep_weight(s)
                if front:
                    for k in turned_ctxs(b, j):
                        keep_ctx(b + 1, k)
                weights(0)
                if ahead and j == 0:
                    norm1(s + 2, j)
                weights(1)
                silus(s, j, 0)
                if ahead and j:
                    norm1(s + 2, j)
                if front and j == 0:
                    norm2(t, j + 1)
                weights(2)
                silus(s, j, 1)
                if front and j:
                    norm2(t, j + 1)
                weights(3)
                silus(s, j, 2)
                if front:
                    keep_z(t, j + 1)
                silus(s, j, 3)
                h_hi(s, j)
                if front:
                    silus(t, j + 1, -1)
                keep_h(s)
                if front:
                    exps(t)

            def weights_of_pair(p):
                for n in range(4 + 2 * p, min(6 + 2 * p, CHUNKS)):
                    if n + 1 < CHUNKS:
                        sum_w(n + 1)
                    split_w(n)

            step(0, 0, (), True, True, weights_of_pair)
            by_round(act, step)

        @block.tensor
        def _(pe):
            HI_LO = ((0, 0), (0, 1), (1, 0))

            def turn_ctx(c, k):
                pe.wait_ge(ctx_round, CTX_ROUNDS * (c + 1))
                wait_at(pe, ctx_kept, c)
                ps = turned[0].bitcast(BF16)
                for kc in range(KC):
                    mm = nc.tensor.transpose(ps[:, kc * P:(kc + 1) * P], ctx_q[:, k % 2, kc * P:(kc + 1) * P], identb[:])
                mm.then_inc(ctx_turned, 1)

            def turn_x(t):
                pe.wait_ge(xq_step, XQ_STEPS * (t + 1))
                ps = turned[1].bitcast(BF16)
                for kc in range(KC):
                    mm = nc.tensor.transpose(ps[:, kc * P:(kc + 1) * P], x_q[:, kc * P:(kc + 1) * P], identb[:])
                mm.then_inc(x_turned, 1)

            def attend(t, b, kc):
                if kc == 0:
                    pe.wait_ge(x_kept, t + 1)
                    pe.wait_ge(ctx_kept, (b + 1) * NB)
                    wait_at(pe, down_read, t)
                elif kc == 1:
                    wait_at(pe, coef_done, t)
                else:
                    pe.wait_ge(att_step, ATT_STEPS * t + (kc - 1) * NB)
                ps = (even_ps, odd_ps)[kc % 2]
                rhs = (ctx_qT[:, b, kc, :] if isinstance(b, int) else
                       ctx_qT[:, bass.ds(b, 1), kc, :].rearrange("p o n -> p (o n)"))
                nc.tensor.matmul(ps[:], x_qT[:, kc, :], rhs, start=True, stop=True).then_inc(att_full, 1)

            def turn_z(t, *parts):
                for h in parts:
                    if h == 0:
                        pe.wait_ge(z_hi_done, t + 1)
                    else:
                        pe.wait_ge(ln_step, LN_STEPS * (t + 1))
                    for kc in range(KC):
                        mm = nc.tensor.transpose(turned[h][:, kc * P:(kc + 1) * P],
                                                 z[h][:, kc * P:(kc + 1) * P], ident16[:])
                    mm.then_inc(z_turned, 1)

            def route(t, j):
                pe.wait_ge(z_kept, 2 * (t + 1))
                if isinstance(t, int) and t == 0:
                    pe.wait_ge(w_ready, 1)
                pe.wait_ge(att_step, ATT_STEPS * (t + 1))
                n = 0
                for kc in range(KC):
                    for a, w in HI_LO:
                        mm = nc.tensor.matmul(odd_ps[:, 0:E], zT[a][:, j % 2, kc, :], wr[w][:, kc, :],
                                              start=(n == 0), stop=(n == 3 * KC - 1))
                        n += 1
                mm.then_inc(logit_full, 1)

            def pair(t, j, p, between={}):
                k, par, n = use(t, p), parity(j, p), chunk(p)
                if 0 in between:
                    between[0]()
                wait_at(pe, pair_read, k)
                for i, (ps, full) in enumerate(((gate_ps[par], gate_full), (up_ps[par], up_full))):
                    if isinstance(t, int) and t == 0:
                        pe.wait_ge(w_ready, n + i + 1)
                    m = 0
                    for kc in range(KC):
                        if i + kc > 0 and KC * i + kc in between:
                            between[KC * i + kc]()
                        for a, w in HI_LO:
                            mm = nc.tensor.matmul(ps[:], zT[a][:, j % 2, kc, :], wgu[w][:, n - 1 + i, kc, :],
                                                  start=(m == 0), stop=(m == 3 * KC - 1))
                            m += 1
                    mm.then_inc(full, 1)

            def turn_h(s, h):
                if h == 0:
                    pe.wait_ge(h_hi_done, s + 1)
                else:
                    pe.wait_ge(hid_step, HID_STEPS * (s + 1))
                for hc in range(HC):
                    mm = nc.tensor.transpose(turned[h][:, hc * P:(hc + 1) * P],
                                             hs[h][:, hc * P:(hc + 1) * P], ident16[:])
                mm.then_inc(h_turned, 1)

            def turn_weight(t):
                pe.wait_ge(top_step, TOP_STEPS * (t + 1) - 2)
                nc.tensor.transpose(odd_ps[:, 0:P], weight[:], ident32[:]).then_inc(weight_turned, 1)

            def coefs(t):
                pe.wait_ge(weightT_kept, t + 1)
                if isinstance(t, int) and t == 0:
                    pe.wait_ge(mix_step, MIX_STEPS)
                nc.tensor.matmul(odd_ps[:, 0:K], weightT[:], mix[:], start=True, stop=True
                                 ).then_inc(coef_full, 1)

            def down(s):
                if isinstance(s, int) and s == 0:
                    pe.wait_ge(w_ready, CHUNKS)
                n = 0
                for a, w in ((0, 0), (0, 1), (1, 0)):
                    if w == 0:
                        pe.wait_ge(h_kept, 2 * s + (a + 1))
                    for hc in range(HC):
                        mm = nc.tensor.matmul(even_ps[:], hT[a][:, hc, :], wd[w][:, hc, :],
                                              start=(n == 0), stop=(n == 3 * HC - 1))
                        n += 1
                mm.then_inc(down_full, 1)

            pe.wait_ge(consts, 3)
            for c in range(NB):
                turn_ctx(c, c)
            turn_x(0)
            for kc in range(KC):
                attend(0, 0, kc)
            turn_z(0, 0, 1)
            route(0, 0)
            pair(0, 0, -1)

            def step(b, j, ctxs, front, ahead):
                s, t = b * NB + j, b * NB + (j + 1)
                bt = b + 1 if j + 1 >= NB else b

                def attends(*kcs):
                    return lambda: [attend(t, bt, kc) for kc in kcs]

                def turn_ctxs():
                    for k in turned_ctxs(b, j):
                        turn_ctx((b + 1) * NB + k, k)

                if not front:
                    for p in range(PAIRS):
                        pair(s, j, p, {0: lambda: turn_weight(s), 3: lambda: coefs(s)} if p == 0 else {})
                    turn_h(s, 0)
                    turn_h(s, 1)
                    down(s)
                    return
                pair(s, j, 0, {0: lambda: (turn_x(t), turn_weight(s)), 3: lambda: coefs(s), 4: turn_ctxs, 6: attends(0, 1)} if j else {0: lambda: (turn_x(t), turn_weight(s), coefs(s), attends(0, 1, 2, 3)())})
                pair(s, j, 1, {2: attends(2, 3)} if j else {})
                pair(s, j, 2, {6: lambda: turn_z(t, 0)})
                pair(s, j, 3, {0: lambda: turn_z(t, 1), 2: lambda: route(t, j + 1)})
                pair(t, j + 1, -1, {7: lambda: turn_h(s, 0)})
                turn_h(s, 1)
                down(s)

            step(0, 0, (), True, True)
            by_round(pe, step)

        @block.vector
        def _(dve):
            dve.sem_inc(pair_read, 1)
            dve.sem_inc(down_read, 1)

            def max_ctx(b, k):
                dve.wait_ge(ctx_loaded[k], 16 * (b + 1))
                nc.vector.tensor_reduce(ctx_max[:, k], ctx_in[:, k, :].rearrange("p (c n) -> p c n", c=KC),
                                        AX.X, ALU.max, apply_absolute_value=True).then_inc(ctx_maxed, 1)

            def scales_ctx(b, k):
                c = b * NB + k
                ch = Chain(dve, ctx_step, CTX_STEPS, c)
                dve.wait_ge(ctx_reduced, c + 1)
                ch.did(nc.vector.tensor_scalar(ctx_safe[:, k], ctx_all[:, k], W_EPS, None, ALU.max))
                ch.sync()
                ch.did(nc.vector.reciprocal(ctx_rec[:, k], ctx_safe[:, k]))
                ch.did(nc.vector.tensor_scalar(ctx_scale[:, bass.ds(c, 1), :].rearrange("p o c -> p (o c)"),
                                               ctx_safe[:, k], 1.0 / FP8_MAX, None, ALU.mult))
                ch.sync(1)
                ch.did(nc.vector.tensor_scalar(ctx_mul[:, k], ctx_rec[:, k], FP8_MAX, None, ALU.mult))
                ch.end()

            def scale_ctx(c, k):
                dve.wait_ge(ctx_step, CTX_STEPS * (c + 1))
                c4 = lambda a: a.rearrange("p (c n) -> p c n", c=KC)
                nc.vector.tensor_tensor(c4(ctx_in[:, k]), c4(ctx_in[:, k]),
                                        ctx_mul[:, k].unsqueeze(2).to_broadcast([P, KC, P]), ALU.mult
                                        ).then_inc(ctx_scaled, 1)

            def mask(ch, v, m):
                ch.did(nc.vector.tensor_scalar(m.bitcast(U32), v.bitcast(U32), EXPONENT, None,
                                               ALU.bitwise_and))
                ch.sync()
                ch.did(nc.vector.tensor_scalar(m, m, FP8_TINY, ROUND, ALU.max, ALU.mult))

            def mask_ctx(b, k):
                c = b * NB + k
                ch = Chain(dve, ctx_mask, CTX_MASKS, c)
                dve.wait_ge(ctx_scaled, c + 1)
                if not isinstance(c, int) or c >= 2:
                    dve.wait_ge(ctx_round, CTX_ROUNDS * (c - 1))
                mask(ch, ctx_in[:, k], ctx_m[:, k % 2])
                ch.end()

            def stats(t, j):
                ch = Chain(dve, stat_step, STAT_STEPS, t)
                dve.wait_ge(x_loaded[j % 2], 16 * ((t - j % 2) // 2 + 1) if isinstance(t, int) else
                            (t - j % 2) * 8 + 16)
                ch.did(nc.vector.bn_stats(stat[:], x_in[:, j % 2, :]))
                ch.sync()
                settle(dve, passed_dve)
                ch.did(nc.vector.bn_aggr(mv[:], stat[:]))
                ch.sync()
                ch.did(nc.vector.tensor_scalar(var[:], mv[:, 1:2], LN_EPS, None, ALU.add))
                ch.did(nc.vector.tensor_scalar(neg_mean[:], mv[:, 0:1], -1.0, None, ALU.mult))
                ch.end()

            def quantise_x(t, b):
                ch = Chain(dve, xq_step, XQ_STEPS, t)
                c4 = lambda a: a.rearrange("p (c n) -> p c n", c=KC)
                dve.wait_ge(y_done, 2 * (t + 1))
                ch.did(nc.vector.tensor_reduce(x_max[:], c4(y[:]), AX.X, ALU.max, apply_absolute_value=True))
                ch.sync()
                ch.did(nc.vector.tensor_scalar(x_safe[:], x_max[:], ACT_EPS, None, ALU.max))
                ch.sync()
                ch.did(nc.vector.reciprocal(x_rec[:], x_safe[:]))
                ch.did(nc.vector.tensor_scalar(x_scale[:], x_safe[:], 1.0 / FP8_MAX, None, ALU.mult))
                ch.sync(1)
                ch.did(nc.vector.tensor_scalar(x_mul[:], x_rec[:], FP8_MAX, None, ALU.mult))
                ch.sync(1)
                dve.wait_ge(ctx_step, CTX_STEPS * (b + 1) * NB)
                ch.did(nc.vector.tensor_tensor(both_scale[:], ctx_scale[:, bass.ds(b * NB, NB), :],
                                               x_scale[:].unsqueeze(1).to_broadcast([P, NB, KC]), ALU.mult))
                ch.sync(1)
                ch.did(nc.vector.tensor_tensor(c4(x_v[:]), c4(y[:]), x_mul[:].unsqueeze(2).to_broadcast([P, KC, P]),
                                               ALU.mult))
                ch.sync()
                mask(ch, x_v[:], x_m[:])
                ch.sync()
                ch.did(nc.vector.tensor_tensor(x_v[:], x_v[:], x_m[:], ALU.add))
                ch.sync()
                wait_at(dve, x_turned, t)
                ch.did(nc.vector.tensor_tensor(x_q[:], x_v[:], x_m[:], ALU.subtract))
                ch.end()

            def attention(t, j):
                dve.wait_ge(xq_step, XQ_STEPS * t + 6)
                ch = Chain(dve, att_step, ATT_STEPS, t)
                for kc in range(KC):
                    dve.wait_ge(att_full, KC * t + (kc + 1))
                    ps = (even_ps, odd_ps)[kc % 2]
                    for nb in range(NB):
                        cols = slice(nb * P, (nb + 1) * P)
                        prev = x_in[:, j % 2, cols] if kc == 0 else x2[:, j % 2, cols]
                        if kc > 0:
                            ch.sync(NB - 1)
                        ch.did(nc.vector.scalar_tensor_tensor(x2[:, j % 2, cols], ps[:, cols],
                                                              both_scale[:, nb, kc:kc + 1], prev,
                                                              ALU.mult, ALU.add))
                ch.end()

            def stats2(t, j):
                ch = Chain(dve, ln_step, LN_STEPS, t)
                dve.wait_ge(att_step, ATT_STEPS * (t + 1))
                ch.did(nc.vector.bn_stats(stat2[:], x2[:, j % 2, :]))
                ch.sync()
                settle(dve, passed_dve)
                ch.did(nc.vector.bn_aggr(mv2[:], stat2[:]))
                ch.sync()
                ch.did(nc.vector.tensor_scalar(var2[:], mv2[:, 1:2], LN_EPS, LN_GAIN ** -2, ALU.add, ALU.mult))
                ch.did(nc.vector.tensor_scalar(neg_mean2[:], mv2[:, 0:1], -1.0, None, ALU.mult))
                return ch

            def z_lo(ch, t):
                dve.wait_ge(y2_done, t + 1)
                dve.wait_ge(z_hi_done, t + 1)
                wait_at(dve, z_turned, 2 * t)
                ch.did(nc.vector.tensor_tensor(z[1][:], y2[:], z[0][:], ALU.subtract))
                ch.end()

            def largest(t):
                ch = Chain(dve, top_step, TOP_STEPS, t)
                dve.wait_ge(logit_full, t + 1)
                ch.did(nc.vector.tensor_scalar(logit[:], odd_ps[:, 0:E], w_back[:, 0:1], None, ALU.mult))
                ch.sync()
                settle(dve, passed_dve)
                ch.did(nc.vector.max(top8[:], logit[:]))
                ch.sync()
                settle(dve, passed_dve)
                ch.did(nc.vector.max_index(idx8[:], top8[:], logit[:]))
                ch.sync()
                ch.did(nc.vector.tensor_copy(idx[:], idx8[:, 0:TOPK]))
                ch.did(nc.vector.tensor_scalar(neg_max[:], top8[:, 0:1], -1.0, None, ALU.mult))
                return ch

            def pick(ch, t):
                ch.sync(1)
                ch.did(nc.vector.tensor_scalar(picked[0][:], iota[:], idx[:, 0:1], None, ALU.is_equal))
                for i in range(1, TOPK):
                    ch.sync()
                    ch.did(nc.vector.scalar_tensor_tensor(picked[i % 2][:], iota[:], idx[:, i:i + 1],
                                                          picked[(i - 1) % 2][:], ALU.is_equal, ALU.add))
                ch.sync()
                dve.wait_ge(exp_done, t + 1)
                ch.did(nc.vector.scalar_tensor_tensor(weight[:], picked[(TOPK - 1) % 2][:], 1.0, prob[:],
                                                      ALU.mult, ALU.mult, accum_out=weight_sum[:]))
                ch.sync()
                ch.did(nc.vector.scalar_tensor_tensor(denom[:], prob_sum[:], TOP_EPS, weight_sum[:],
                                                      ALU.mult, ALU.add))
                ch.sync()
                ch.did(nc.vector.reciprocal(inv_denom[:], denom[:]))
                ch.end()

            def coefficients(t):
                dve.wait_ge(coef_full, t + 1)
                dve.wait_ge(top_step, TOP_STEPS * (t + 1))
                nc.vector.tensor_scalar(coef[:], odd_ps[:, 0:K], inv_denom[:], None, ALU.mult
                                        ).then_inc(coef_done, 1)

            def combine(t, j, p):
                k, par, n = use(t, p), parity(j, p), chunk(p) + 1
                dve.wait_ge(up_full, k + 1)
                dve.wait_ge(silu_done, k + 1)
                dst = hid[:, j % 2, I:HW] if p < 0 else basis[:]
                if p > 0:
                    dve.wait_ge(mix_acc, MIX_ACC * t + KPC * p)
                nc.vector.scalar_tensor_tensor(dst, up_ps[par][:], w_back[:, n:n + 1], silu[:, par, :],
                                               ALU.mult, ALU.mult).then_inc(pair_read, 1)
                if p < 0:
                    dve.wait_ge(pair_read, k + 2)
                    nc.vector.tensor_reduce(shared_top[:, 0:1], hid[:, j % 2, I:HW], AX.X, ALU.max,
                                            apply_absolute_value=True).then_inc(shared_max, 1)
                    return
                dve.wait_ge(pair_read, k + 2)
                dve.wait_ge(coef_done, t + 1)
                mixed = hid[:, j % 2, 0:I]
                for i in range(KPC):
                    kk = p * KPC + i
                    part = basis[:, i * I:(i + 1) * I]
                    if kk == 0:
                        ins = nc.vector.tensor_scalar(mixed, part, coef[:, 0:1], None, ALU.mult)
                    else:
                        dve.wait_ge(mix_acc, MIX_ACC * t + kk)
                        ins = nc.vector.scalar_tensor_tensor(mixed, part, coef[:, kk:kk + 1], mixed,
                                                             ALU.mult, ALU.add)
                    ins.then_inc(mix_acc, 1)

            def scale_h(s, j):
                ch = Chain(dve, hid_step, HID_STEPS, s)
                dve.wait_ge(mix_acc, MIX_ACC * (s + 1))
                dve.wait_ge(shared_max, s + 1)
                ch.did(nc.vector.tensor_scalar(hid_max[:, 0:1], shared_top[:], SMALLEST, None, ALU.max))
                ch.did(nc.vector.tensor_reduce(hid_max[:, 1:2], hid[:, j % 2, 0:I], AX.X, ALU.max,
                                               apply_absolute_value=True))
                ch.sync()
                ch.did(nc.vector.tensor_scalar(hid_tmp[:], hid_max[:, 1:2], hid_max[:, 0:1], TO_2_14,
                                               ALU.max, ALU.mult))
                ch.sync()
                ch.did(nc.vector.tensor_scalar(hid_unscale[:].bitcast(U32), hid_tmp[:].bitcast(U32),
                                               EXPONENT, None, ALU.bitwise_and))
                ch.sync()
                ch.did(nc.vector.reciprocal(hid_scale[:], hid_unscale[:]))
                return ch

            def split_h(ch, s, j):
                dve.wait_ge(h_hi_done, s + 1)
                ch.sync()
                ch.did(nc.vector.scalar_tensor_tensor(hs[1][:], hid[:, j % 2, :], hid_scale[:], hs[0][:],
                                                      ALU.mult, ALU.subtract))
                ch.end()

            def finish(s, j):
                nc.vector.tensor_tensor(out_scale[:], hid_unscale[:], w_unscale[:, DOWN:DOWN + 1], ALU.mult
                                        ).then_inc(out_scaled, 1)
                dve.wait_ge(down_full, s + 1)
                dve.wait_ge(out_scaled, s + 1)
                dve.wait_ge(stored[j % 2], (s - j % 2) * 8 + 16)
                nc.vector.scalar_tensor_tensor(y_out[:, j % 2, :], even_ps[:], out_scale[:], x2[:, j % 2, :],
                                               ALU.mult, ALU.add).then_inc(down_read, 1)

            def max_w(n):
                if n not in MAX_BY_DVE:
                    return
                wait_staged(dve, n)
                nc.vector.tensor_reduce(w_max[:, n:n + 1], w_staged(n), AX.X, ALU.max,
                                        apply_absolute_value=True).then_inc(w_maxed, 1)

            def scale_w(n):
                ch = Chain(dve, w_step, W_STEPS, n)
                one = slice(n, n + 1)
                dve.wait_ge(w_reduced, n + 1)
                ch.did(nc.vector.tensor_scalar(w_tmp[:, one], w_all[:, one], SMALLEST, TO_2_14,
                                               ALU.max, ALU.mult))
                ch.sync()
                ch.did(nc.vector.tensor_scalar(w_unscale[:, one].bitcast(U32), w_tmp[:, one].bitcast(U32),
                                               EXPONENT, None, ALU.bitwise_and))
                ch.sync()
                ch.did(nc.vector.reciprocal(w_scale[:, one], w_unscale[:, one]))
                ch.did(nc.vector.tensor_scalar(w_back[:, one], w_unscale[:, one], 1.0 / LN_GAIN, None, ALU.mult))
                ch.end()

            def lo_w(n):
                dve.wait_ge(w_hi_done, n + 1)
                dve.wait_ge(w_step, W_STEPS * (n + 1))
                nc.vector.scalar_tensor_tensor(w_part(1, n), w_staged(n), w_scale[:, n:n + 1], w_part(0, n),
                                               ALU.mult, ALU.subtract).then_inc(w_ready, 1)

            def mixes():
                ch = Chain(dve, mix_step, MIX_STEPS, 0)
                dve.wait_ge(small_in, 32)
                ch.did(nc.vector.tensor_tensor(amp_sq[:], amp[:], amp[:], ALU.mult))
                ch.sync()
                ch.did(nc.vector.tensor_tensor(power[:], amp_sq[:, :, 0], amp_sq[:, :, 1], ALU.add))
                ch.sync()
                ch.did(nc.vector.tensor_reduce(power_sum[:, 0:1], power[:], AX.X, ALU.add))
                ch.sync()
                ch.did(nc.vector.tensor_scalar(power_sum[:, 0:1], power_sum[:, 0:1], TOP_EPS, None, ALU.add))
                ch.sync()
                ch.did(nc.vector.reciprocal(power_sum[:, 1:2], power_sum[:, 0:1]))
                ch.sync()
                ch.did(nc.vector.tensor_scalar(mix[:], power[:], power_sum[:, 1:2], escale[:],
                                               ALU.mult, ALU.mult))
                ch.end()

            dve.wait_ge(made, 4)
            nc.vector.tensor_copy(identb[:], ident32[:]).then_inc(consts, 1)
            nc.vector.tensor_copy(ident16[:], ident32[:]).then_inc(consts, 1)
            nc.vector.tensor_copy(iota[:], iota_i[:]).then_inc(consts, 1)
            max_ctx(0, 0)
            stats(0, 0)
            max_ctx(0, 1)
            scales_ctx(0, 0)
            scale_ctx(0, 0)
            mask_ctx(0, 0)
            scales_ctx(0, 1)
            scale_ctx(1, 1)
            mask_ctx(0, 1)
            max_ctx(0, 2)
            max_ctx(0, 3)
            scale_w(0)
            scales_ctx(0, 2)
            scales_ctx(0, 3)
            mask_ctx(0, 2)
            quantise_x(0, 0)
            mask_ctx(0, 3)
            mixes()
            lo_w(0)
            scale_w(1)
            scale_w(2)
            lo_w(1)
            attention(0, 0)
            ln = stats2(0, 0)
            stats(1, 1)
            scale_w(3)
            lo_w(2)
            z_lo(ln, 0)
            quantise_x(1, 0)
            scale_w(4)
            lo_w(3)
            pick(largest(0), 0)
            combine(0, 0, -1)

            def step(b, j, ctxs, front, ahead, weights=lambda p: None):
                s, t = b * NB + j, b * NB + (j + 1)
                bu = b + 1 if j + 2 >= NB else b
                for k in ctxs:
                    max_ctx(b + 1, k)
                if ahead:
                    stats(s + 2, j)
                coefficients(s)
                weights(0)
                for k in ctxs:
                    scales_ctx(b + 1, k)
                if front:
                    attention(t, j + 1)
                if front and j == 0:
                    ln = stats2(t, j + 1)
                weights(1)
                combine(s, j, 0)
                if front and j:
                    ln = stats2(t, j + 1)
                if j:
                    combine(s, j, 1)
                if front:
                    z_lo(ln, t)
                for k in ctxs[:1]:
                    mask_ctx(b + 1, k)
                if ahead:
                    quantise_x(s + 2, bu)
                weights(2)
                if j == 0:
                    combine(s, j, 1)
                weights(3)
                combine(s, j, 2)
                combine(s, j, 3)
                hid_chain = scale_h(s, j)
                if front:
                    top_chain = largest(t)
                split_h(hid_chain, s, j)
                for k in ctxs[1:]:
                    mask_ctx(b + 1, k)
                if front:
                    pick(top_chain, t)
                if front:
                    combine(t, j + 1, -1)
                finish(s, j)

            def split_weights(p):
                for n in range(4 + 2 * p, min(6 + 2 * p, CHUNKS)):
                    if n + 1 < CHUNKS:
                        max_w(n + 1)
                        scale_w(n + 1)
                    lo_w(n)

            step(0, 0, (), True, True, split_weights)
            by_round(dve, step)


_INS = ["x", "ctx_2048", "L0_ffn_w_router", "L0_ffn_w_gate", "L0_ffn_w_up", "L0_ffn_w_down",
        "L0_ffn_amplitudes", "L0_ffn_expert_scale", "L0_ffn_shared_w_gate", "L0_ffn_shared_w_up",
        "L0_ffn_shared_w_down"]


def kernel(**inputs):
    import numpy as _np
    import concourse.bacc as _bacc
    from concourse import mybir as _mybir
    from concourse.bass_utils import run_bass_kernel_spmd as _run

    nc = _bacc.Bacc("TRN2", target_bir_lowering=False, num_devices=1)
    arrays, args = {}, []
    for name in _INS:
        a = _np.ascontiguousarray(inputs[name])
        arrays[f"in_{name}"] = a
        args.append(nc.dram_tensor(f"in_{name}", a.shape, _mybir.dt.from_np(a.dtype), kind="ExternalInput").ap())
    x = inputs["x"]
    args.append(nc.dram_tensor("out_0", x.shape, _mybir.dt.float32, kind="ExternalOutput").ap())
    build(nc, *args)
    r = _run(nc, [arrays], core_ids=[0])
    return r.results[0]["out_0"]
```
